# Optimizing a Trainium2 kernel written in Bass

```python
import numpy as np
import jax
import jax.numpy as jnp

def _softmax(x, axis=-1):
    return jax.nn.softmax(x, axis=axis)
def _gelu(x):
    return jax.nn.gelu(x, approximate=True)
def _silu(x):
    return jax.nn.silu(x)
def _sigmoid(x):
    return jax.nn.sigmoid(x)
def _layernorm(x, axis=-1, eps=1e-5):
    m = jnp.mean(x, axis=axis, keepdims=True)
    v = jnp.var(x, axis=axis, keepdims=True)
    return (x - m) / jnp.sqrt(v + eps)
def _scatter_add(tgt, idx, src, axis=0):
    return tgt.at[idx].add(src)
def _segment_sum(src, seg, n):
    return jax.ops.segment_sum(src, seg, n)

kernel_name = 'mk_conv_seq_d4_conv_nhwc256_64f758'

def setup_inputs(seed: int = 0):
    np.random.seed(seed)
    _w = jnp.asarray
    def _rec_inputs():
        import jax
        import jax.numpy as jnp
        _gk = jax.random.key(seed)
        x = -0.0005207 + 1.001 * jax.random.normal(jax.random.fold_in(_gk, 1), (2, 64, 64, 256), jnp.float32)
        return x
    x = _rec_inputs()
    def _L0_conv_setup():
        import jax, jax.numpy as jnp
        import numpy as np
        NUM_HEADS = 8

        def layer_norm(x, g, b, eps=1e-05):
            m = x.mean(-1, keepdims=True)
            v = ((x - m) ** 2).mean(-1, keepdims=True)
            return (x - m) / jnp.sqrt(v + eps) * g + b
        D, B, N = (256, 2, 64)
        key = jax.random.key(seed)
        ks = jax.random.split(key, 9)
        s = 0.02
        return {'x': jax.random.normal(ks[0], (B, N, N, D), jnp.float32), 'Wq': jax.random.normal(ks[1], (D, D), jnp.float32) * s, 'Wk': jax.random.normal(ks[2], (D, D), jnp.float32) * s, 'Wv1': jax.random.normal(ks[3], (D, D), jnp.float32) * s, 'Wv2': jax.random.normal(ks[4], (D, D), jnp.float32) * s, 'Wo': jax.random.normal(ks[5], (D, D), jnp.float32) * s, 'W1': jax.random.normal(ks[6], (D, 2 * D), jnp.float32) * s, 'b1': jnp.zeros((2 * D,), jnp.float32), 'W2': jax.random.normal(ks[7], (2 * D, D), jnp.float32) * s, 'b2': jnp.zeros((D,), jnp.float32), 'g_agg': jnp.ones((D,), jnp.float32), 'be_agg': jnp.zeros((D,), jnp.float32), 'g_out': jnp.ones((D,), jnp.float32), 'be_out': jnp.zeros((D,), jnp.float32)}
    _L0_conv_all = _L0_conv_setup()
    _L0_conv_in = {k: v for k, v in _L0_conv_all.items() if k in ('Wq', 'Wk', 'Wv1', 'Wv2', 'Wo', 'W1', 'b1', 'W2', 'b2', 'g_agg', 'be_agg', 'g_out', 'be_out', )}
    del _L0_conv_all

    def _L1_conv_setup():
        import jax, jax.numpy as jnp
        import numpy as np
        CH = 256
        CFG = CH // 8
        key = jax.random.key(seed)
        k1, k2, k3, k4, k5 = jax.random.split(key, 5)
        B, H, W, C = (4, 64, 64, CH)
        std = 0.04
        x = jax.random.normal(k1, (B, H, W, C), dtype=jnp.float32)
        kernel_f = jax.random.normal(k2, (C, CFG), dtype=jnp.float32) * std
        kernel_g = jax.random.normal(k3, (C, CFG), dtype=jnp.float32) * std
        kernel_h = jax.random.normal(k4, (C, C), dtype=jnp.float32) * std
        gamma = jax.random.normal(k5, (1,), dtype=jnp.float32) * std
        return {'x': x, 'kernel_f': kernel_f, 'kernel_g': kernel_g, 'kernel_h': kernel_h, 'gamma': gamma}
    _L1_conv_all = _L1_conv_setup()
    _L1_conv_in = {k: v for k, v in _L1_conv_all.items() if k in ('kernel_f', 'kernel_g', 'kernel_h', 'gamma', )}
    del _L1_conv_all

    def _L2_conv_setup():
        import jax, jax.numpy as jnp
        import numpy as np

        def conv1x1(x, W, b):
            return jnp.einsum('bhwc,cd->bhwd', x, W) + b
        key = jax.random.key(seed)
        ks = jax.random.split(key, 8)
        B, H, W, C, Cr = (8, 64, 64, 256, 16)
        s = 0.05
        return {'x': jax.random.normal(ks[0], (B, H, W, C), jnp.float32), 'Wq': jax.random.normal(ks[1], (C, Cr), jnp.float32) * s, 'bq': jnp.zeros((Cr,), jnp.float32), 'Wk': jax.random.normal(ks[2], (C, Cr), jnp.float32) * s, 'bk': jnp.zeros((Cr,), jnp.float32), 'Wv': jax.random.normal(ks[3], (C, C), jnp.float32) * s, 'bv': jnp.zeros((C,), jnp.float32), 'Wcq': jax.random.normal(ks[4], (C, Cr), jnp.float32) * s, 'bcq': jnp.zeros((Cr,), jnp.float32), 'Wck': jax.random.normal(ks[5], (C, Cr), jnp.float32) * s, 'bck': jnp.zeros((Cr,), jnp.float32), 'Wcv': jax.random.normal(ks[6], (C, Cr), jnp.float32) * s, 'bcv': jnp.zeros((Cr,), jnp.float32), 'Wp': jax.random.normal(ks[7], (Cr, C), jnp.float32) * s, 'bp': jnp.zeros((C,), jnp.float32)}
    _L2_conv_all = _L2_conv_setup()
    _L2_conv_in = {k: v for k, v in _L2_conv_all.items() if k in ('Wq', 'bq', 'Wk', 'bk', 'Wv', 'bv', 'Wcq', 'bcq', 'Wck', 'bck', 'Wcv', 'bcv', 'Wp', 'bp', )}
    del _L2_conv_all

    def _L3_conv_setup():
        import jax, jax.numpy as jnp
        import numpy as np
        from jax import lax
        KH = 3
        K = KH * KH
        BN_EPS = 0.001

        def _conv3x3_same(x, w):
            return lax.conv_general_dilated(x, w, window_strides=(1, 1), padding='SAME', dimension_numbers=('NHWC', 'HWIO', 'NHWC'))
        key = jax.random.key(seed)
        k0, k1, k2, k3, k4 = jax.random.split(key, 5)
        B, H, W, C, F = (4, 64, 64, 256, 256)
        x = jax.random.normal(k0, (B, H, W, C), jnp.float32)
        offset_w = jax.random.normal(k1, (3, 3, C, 3 * K), jnp.float32) * 0.01
        dcn_w = jax.random.normal(k2, (3, 3, C, F), jnp.float32) * np.sqrt(2.0 / (K * C)).astype(np.float32)
        gamma = jnp.ones((F,), jnp.float32)
        beta = jnp.zeros((F,), jnp.float32)
        moving_mean = jax.random.normal(k3, (F,), jnp.float32) * 0.1
        moving_var = jax.random.uniform(k4, (F,), jnp.float32, 0.5, 1.5)
        return dict(x=x, offset_w=offset_w, dcn_w=dcn_w, gamma=gamma, beta=beta, moving_mean=moving_mean, moving_var=moving_var)
    _L3_conv_all = _L3_conv_setup()
    _L3_conv_in = {k: v for k, v in _L3_conv_all.items() if k in ('offset_w', 'dcn_w', 'gamma', 'beta', 'moving_mean', 'moving_var', )}
    del _L3_conv_all

    return {
        "x": x,
        "L0_conv_Wq": _L0_conv_in["Wq"],
        "L0_conv_Wk": _L0_conv_in["Wk"],
        "L0_conv_Wv1": _L0_conv_in["Wv1"],
        "L0_conv_Wv2": _L0_conv_in["Wv2"],
        "L0_conv_Wo": _L0_conv_in["Wo"],
        "L0_conv_W1": _L0_conv_in["W1"],
        "L0_conv_b1": _L0_conv_in["b1"],
        "L0_conv_W2": _L0_conv_in["W2"],
        "L0_conv_b2": _L0_conv_in["b2"],
        "L0_conv_g_agg": _L0_conv_in["g_agg"],
        "L0_conv_be_agg": _L0_conv_in["be_agg"],
        "L0_conv_g_out": _L0_conv_in["g_out"],
        "L0_conv_be_out": _L0_conv_in["be_out"],
        "L1_conv_kernel_f": _L1_conv_in["kernel_f"],
        "L1_conv_kernel_g": _L1_conv_in["kernel_g"],
        "L1_conv_kernel_h": _L1_conv_in["kernel_h"],
        "L1_conv_gamma": _L1_conv_in["gamma"],
        "L2_conv_Wq": _L2_conv_in["Wq"],
        "L2_conv_bq": _L2_conv_in["bq"],
        "L2_conv_Wk": _L2_conv_in["Wk"],
        "L2_conv_bk": _L2_conv_in["bk"],
        "L2_conv_Wv": _L2_conv_in["Wv"],
        "L2_conv_bv": _L2_conv_in["bv"],
        "L2_conv_Wcq": _L2_conv_in["Wcq"],
        "L2_conv_bcq": _L2_conv_in["bcq"],
        "L2_conv_Wck": _L2_conv_in["Wck"],
        "L2_conv_bck": _L2_conv_in["bck"],
        "L2_conv_Wcv": _L2_conv_in["Wcv"],
        "L2_conv_bcv": _L2_conv_in["bcv"],
        "L2_conv_Wp": _L2_conv_in["Wp"],
        "L2_conv_bp": _L2_conv_in["bp"],
        "L3_conv_offset_w": _L3_conv_in["offset_w"],
        "L3_conv_dcn_w": _L3_conv_in["dcn_w"],
        "L3_conv_gamma": _L3_conv_in["gamma"],
        "L3_conv_beta": _L3_conv_in["beta"],
        "L3_conv_moving_mean": _L3_conv_in["moving_mean"],
        "L3_conv_moving_var": _L3_conv_in["moving_var"],
    }

def reference(x, L0_conv_Wq, L0_conv_Wk, L0_conv_Wv1, L0_conv_Wv2, L0_conv_Wo, L0_conv_W1, L0_conv_b1, L0_conv_W2, L0_conv_b2, L0_conv_g_agg, L0_conv_be_agg, L0_conv_g_out, L0_conv_be_out, L1_conv_kernel_f, L1_conv_kernel_g, L1_conv_kernel_h, L1_conv_gamma, L2_conv_Wq, L2_conv_bq, L2_conv_Wk, L2_conv_bk, L2_conv_Wv, L2_conv_bv, L2_conv_Wcq, L2_conv_bcq, L2_conv_Wck, L2_conv_bck, L2_conv_Wcv, L2_conv_bcv, L2_conv_Wp, L2_conv_bp, L3_conv_offset_w, L3_conv_dcn_w, L3_conv_gamma, L3_conv_beta, L3_conv_moving_mean, L3_conv_moving_var):
    import jax
    import jax.numpy as jnp
    def _L0_conv_ref(x, Wq, Wk, Wv1, Wv2, Wo, W1, b1, W2, b2, g_agg, be_agg, g_out, be_out):
        import jax, jax.numpy as jnp
        import numpy as np
        NUM_HEADS = 8

        def layer_norm(x, g, b, eps=1e-05):
            m = x.mean(-1, keepdims=True)
            v = ((x - m) ** 2).mean(-1, keepdims=True)
            return (x - m) / jnp.sqrt(v + eps) * g + b
        B, N, _, D = x.shape
        H = NUM_HEADS
        dk = D // H
        q = (x @ Wq).reshape(B, N, N, H, dk)
        k = (x @ Wk).reshape(B, N, N, H, dk)
        v1 = (x @ Wv1).reshape(B, N, N, H, dk)
        v2 = (x @ Wv2).reshape(B, N, N, H, dk)
        scores = jnp.einsum('bijhd,bjlhd->bijlh', q, k) / jnp.sqrt(jnp.float32(dk))
        att = jax.nn.softmax(scores, axis=2)
        out = jnp.einsum('bijlh,bijhd,bjlhd->bilhd', att, v1, v2)
        attn_out = out.reshape(B, N, N, D) @ Wo
        h = layer_norm(x + attn_out, g_agg, be_agg)
        h = layer_norm(jax.nn.relu(h @ W1 + b1) @ W2 + b2 + h, g_out, be_out)
        return h

    def _L1_conv_ref(x, kernel_f, kernel_g, kernel_h, gamma):
        import jax, jax.numpy as jnp
        import numpy as np
        CH = 256
        CFG = CH // 8
        B, H, W, C = x.shape
        N = H * W
        xf = x.reshape(B, N, C)
        f = jnp.einsum('bnc,cd->bnd', xf, kernel_f)
        g = jnp.einsum('bnc,cd->bnd', xf, kernel_g)
        h = jnp.einsum('bnc,cd->bnd', xf, kernel_h)
        s = jnp.einsum('bnd,bmd->bnm', g, f)
        beta = jax.nn.softmax(s, axis=-1)
        o = jnp.einsum('bnm,bmc->bnc', beta, h)
        o = o.reshape(B, H, W, C)
        return gamma * o + x

    def _L2_conv_ref(x, Wq, bq, Wk, bk, Wv, bv, Wcq, bcq, Wck, bck, Wcv, bcv, Wp, bp):
        import jax, jax.numpy as jnp
        import numpy as np

        def conv1x1(x, W, b):
            return jnp.einsum('bhwc,cd->bhwd', x, W) + b
        B, H, W, C = x.shape
        Cr = Wq.shape[1]
        N = H * W
        scale = jnp.sqrt(jnp.asarray(Cr, x.dtype))
        q = conv1x1(x, Wq, bq).reshape(B, N, Cr)
        k = conv1x1(x, Wk, bk).reshape(B, N, Cr)
        v = conv1x1(x, Wv, bv).reshape(B, N, C)
        pos_scores = jnp.einsum('bnc,bmc->bnm', q, k) / scale
        pos_attn = jax.nn.softmax(pos_scores, axis=-1)
        pos_out = jnp.einsum('bnm,bmc->bnc', pos_attn, v).reshape(B, H, W, C)
        cq = conv1x1(x, Wcq, bcq).reshape(B, N, Cr)
        ck = conv1x1(x, Wck, bck).reshape(B, N, Cr)
        cv = conv1x1(x, Wcv, bcv).reshape(B, N, Cr)
        chan_scores = jnp.einsum('bnc,bnd->bcd', ck, cq) / scale
        chan_attn = jax.nn.softmax(chan_scores, axis=-1)
        chan_out = jnp.einsum('bcd,bnd->bnc', chan_attn, cv).reshape(B, H, W, Cr)
        chan_out = conv1x1(chan_out, Wp, bp)
        return x + pos_out + chan_out

    def _L3_conv_ref(x, offset_w, dcn_w, gamma, beta, moving_mean, moving_var):
        import jax, jax.numpy as jnp
        import numpy as np
        from jax import lax
        KH = 3
        K = KH * KH
        BN_EPS = 0.001

        def _conv3x3_same(x, w):
            return lax.conv_general_dilated(x, w, window_strides=(1, 1), padding='SAME', dimension_numbers=('NHWC', 'HWIO', 'NHWC'))
        B, H, W, C = x.shape
        F = dcn_w.shape[-1]
        off = _conv3x3_same(x, offset_w)
        dy = off[..., :K]
        dx = off[..., K:2 * K]
        mask = jax.nn.sigmoid(off[..., 2 * K:])
        ii = jnp.arange(H, dtype=x.dtype)[None, :, None, None]
        jj = jnp.arange(W, dtype=x.dtype)[None, None, :, None]
        ky = jnp.array([-1, -1, -1, 0, 0, 0, 1, 1, 1], x.dtype)
        kx = jnp.array([-1, 0, 1, -1, 0, 1, -1, 0, 1], x.dtype)
        py = ii + ky + dy
        px = jj + kx + dx
        y0 = jnp.floor(py)
        x0 = jnp.floor(px)
        wy1 = py - y0
        wx1 = px - x0
        wy0 = 1.0 - wy1
        wx0 = 1.0 - wx1
        y0i = y0.astype(jnp.int32)
        x0i = x0.astype(jnp.int32)
        y1i = y0i + 1
        x1i = x0i + 1
        b_idx = jnp.arange(B)[:, None, None, None]

        def gather(yi, xi):
            valid = (yi >= 0) & (yi < H) & (xi >= 0) & (xi < W)
            yc = jnp.clip(yi, 0, H - 1)
            xc = jnp.clip(xi, 0, W - 1)
            v = x[b_idx, yc, xc]
            return v * valid[..., None].astype(x.dtype)
        val = gather(y0i, x0i) * (wy0 * wx0)[..., None] + gather(y0i, x1i) * (wy0 * wx1)[..., None] + gather(y1i, x0i) * (wy1 * wx0)[..., None] + gather(y1i, x1i) * (wy1 * wx1)[..., None]
        sampled = val * mask[..., None]
        out = jnp.einsum('bhwkc,kcf->bhwf', sampled, dcn_w.reshape(K, C, F))
        inv = gamma * lax.rsqrt(moving_var + BN_EPS)
        out = (out - moving_mean) * inv + beta
        return jax.nn.relu(out)

    def _gn(v, G=32, eps=1e-5):
        B_, H_, W_, C_ = v.shape
        g = v.reshape(B_, H_, W_, G, C_ // G)
        m = jnp.mean(g, axis=(1, 2, 4), keepdims=True)
        s = jnp.var(g, axis=(1, 2, 4), keepdims=True)
        return ((g - m) / jnp.sqrt(s + eps)).reshape(v.shape)

    def _ln_c(v, eps=1e-6):
        m = jnp.mean(v, axis=-1, keepdims=True)
        s = jnp.var(v, axis=-1, keepdims=True)
        return (v - m) / jnp.sqrt(s + eps)

    def _ln_t(v, eps=1e-5):
        m = jnp.mean(v, axis=-1, keepdims=True)
        s = jnp.var(v, axis=-1, keepdims=True)
        return (v - m) / jnp.sqrt(s + eps)

    def _to_tokens(v):
        B_, H_, W_, C_ = v.shape
        return v.reshape(B_, H_ * W_, C_)
    def _from_tokens(t, like):
        return t.reshape(like.shape)

    x = _L0_conv_ref(x, L0_conv_Wq, L0_conv_Wk, L0_conv_Wv1, L0_conv_Wv2, L0_conv_Wo, L0_conv_W1, L0_conv_b1, L0_conv_W2, L0_conv_b2, L0_conv_g_agg, L0_conv_be_agg, L0_conv_g_out, L0_conv_be_out)
    x = _L1_conv_ref(x, L1_conv_kernel_f, L1_conv_kernel_g, L1_conv_kernel_h, L1_conv_gamma)
    x = _L2_conv_ref(x, L2_conv_Wq, L2_conv_bq, L2_conv_Wk, L2_conv_bk, L2_conv_Wv, L2_conv_bv, L2_conv_Wcq, L2_conv_bcq, L2_conv_Wck, L2_conv_bck, L2_conv_Wcv, L2_conv_bcv, L2_conv_Wp, L2_conv_bp)
    x = _L3_conv_ref(x, L3_conv_offset_w, L3_conv_dcn_w, L3_conv_gamma, L3_conv_beta, L3_conv_moving_mean, L3_conv_moving_var)
    return x


_drawn_inputs = setup_inputs


def setup_inputs(seed=0):
    import zlib

    import numpy as np

    out = dict(_drawn_inputs(seed))
    spreads = {'L0_conv_b1': (0.0, 0.1),
     'L0_conv_b2': (0.0, 0.1),
     'L0_conv_g_agg': (1.0, 0.2),
     'L0_conv_be_agg': (0.0, 0.1),
     'L0_conv_g_out': (1.0, 0.2),
     'L0_conv_be_out': (0.0, 0.1),
     'L2_conv_bq': (0.0, 0.8),
     'L2_conv_bk': (0.0, 0.8),
     'L2_conv_bv': (0.0, 0.1),
     'L2_conv_bcq': (0.0, 0.1),
     'L2_conv_bck': (0.0, 0.1),
     'L2_conv_bcv': (0.0, 0.329),
     'L2_conv_bp': (0.0, 0.1),
     'L3_conv_gamma': (1.0, 0.2),
     'L3_conv_beta': (0.0, 0.1)}
    factors = {'L0_conv_Wq': 8.0,
     'L0_conv_Wk': 8.0,
     'L0_conv_Wv1': 8.0,
     'L0_conv_Wv2': 8.0,
     'L0_conv_Wo': 8.0,
     'L1_conv_kernel_f': 4.734,
     'L1_conv_kernel_g': 3.642,
     'L1_conv_kernel_h': 3.71}
    for name, (base, spread) in spreads.items():
        noise = np.random.default_rng([zlib.crc32(name.encode()), seed]).standard_normal(out[name].shape)
        drawn = base * np.exp(spread * noise) if base else spread * noise
        out[name] = jnp.asarray(drawn.astype(out[name].dtype))
    for name, factor in factors.items():
        out[name] = (out[name] * factor).astype(out[name].dtype)
    return out
```

```python
from contextlib import ExitStack

import concourse.bass as bass
from concourse import mybir

F32 = mybir.dt.float32
F32R = mybir.dt.float32r
I32 = mybir.dt.int32
U32 = mybir.dt.uint32
ACT = mybir.ActivationFunctionType
ALU = mybir.AluOpType
AX = mybir.AxisListType

P = 128
B = 2
N = 64
C = 256
KC = C // P
HW = N * N
T = B * HW
BANK = 512
HEADS = 8
DK = C // HEADS
FF = 2 * C
KF = FF // P


def wait(eng, sem, count):
    if not (isinstance(count, int) and count <= 0):
        eng.wait_ge(sem, count)


def turns(eng, count, step, unroll=2, head=1, tail=1):
    rounds = count // unroll
    for r in range(head):
        for u in range(unroll):
            step(r * unroll + u, r, u)
    with eng.Fori(head, rounds - tail) as r:
        for u in range(unroll):
            step(r * unroll + u, r, u)
    for r in range(rounds - tail, rounds):
        for u in range(unroll):
            step(r * unroll + u, r, u)


def rows(w):
    return w.rearrange("(k p) n -> p k n", p=P)


def column(v):
    return v.rearrange("(p a) -> p a", a=1)


def across(v, parts=P):
    return v.rearrange("(a n) -> a n", a=1).broadcast_to([parts, v.shape[0]])


class Chip:

    def __init__(self, nc, ctx):
        self.nc, self.ctx, self.part = nc, ctx, ""
        self.psum = ctx.enter_context(nc.psum_tensor("psum", [P, 8, BANK], F32))
        self.ident = ctx.enter_context(nc.sbuf_tensor("ident", [P, P], F32))

    def sem(self, name):
        return self.nc.alloc_semaphore(name=f"{self.part}_{name}")


def make_identity(nc, chip):
    chip.part = "start"
    zeroed, identity_ready, cleared = (chip.sem(n) for n in ("zeroed", "identity_ready", "psum_cleared"))
    with nc.Block() as block:
        @block.gpsimd
        def _(pool):
            nc.gpsimd.memset(chip.ident[:], 0.0).then_inc(zeroed, 1)
            pool.wait_ge(zeroed, 1)
            nc.gpsimd.affine_select(out=chip.ident[:], in_=chip.ident[:], compare_op=ALU.not_equal, fill=1.0,
                                    base=0, pattern=[[-1, P]], channel_multiplier=1).then_inc(identity_ready, 1)
            pool.wait_ge(identity_ready, 1)

        @block.vector
        def _(dve):
            nc.vector.memset(chip.psum[:], 0.0).then_inc(cleared, 1)
            dve.wait_ge(cleared, 1)


def triangle_scores(nc, chip, x, wq, wk, wv2, v2_dram, e_dram, r_dram):
    chip.part = "scores"
    psum = chip.psum
    with ExitStack() as ctx:
        def sb(name, shape, dt=F32):
            return ctx.enter_context(nc.sbuf_tensor(name, shape, dt))

        wq_sb, wk_sb, wv_sb = sb("wq_sb", [P, KC, C]), sb("wk_sb", [P, KC, C]), sb("wv2_sb", [P, KC, C])
        x_in = sb("x_in", [P, 2, 2, C])
        xT = sb("xT", [P, 2, KC, P])
        qk = sb("qk", [P, 4, P])
        v_out = sb("v_out", [P, 2, C])
        S = sb("S", [P, N, BANK])
        top = sb("top", [P, BANK])
        part_sum = sb("part_sum", [P, 4, BANK])
        denom = sb("denom", [P, BANK])
        inverse = sb("inverse", [P, BANK])

        weights = chip.sem("weights")
        loaded = [chip.sem(f"loaded{u}") for u in range(2)]
        stored = [chip.sem(f"stored{u}") for u in range(2)]
        transposed, xT_copied = chip.sem("transposed"), chip.sem("xT_copied")
        qk_done, qk_copied = chip.sem("qk_done"), chip.sem("qk_copied")
        v_done, v_copied = chip.sem("v_done"), chip.sem("v_copied")
        scores_done, scores_copied, maxed = chip.sem("scores_done"), chip.sem("scores_copied"), chip.sem("maxed")

        with nc.Block() as block:
            @block.sync
            def _(sp):
                for w, dst in ((wq, wq_sb), (wk, wk_sb), (wv2, wv_sb)):
                    sp.dma_start(dst[:], rows(w)).then_inc(weights, 16)

                def load(s, u):
                    for b in range(B):
                        half = slice(b * N, (b + 1) * N)
                        sp.dma_start(x_in[half, u, 0, :], x[b, s]).then_inc(loaded[u], 16)
                        sp.dma_start(x_in[half, u, 1, :], x[b, :, s]).then_inc(loaded[u], 16)

                def step(s, r, u, more=True):
                    if more:
                        sp.wait_ge(transposed, s + 1)
                        load(s + 2, u)
                    sp.wait_ge(v_copied, s + 1)
                    sp.dma_start(v2_dram[s], v_out[:, u, :]).then_inc(stored[u], 16)

                load(0, 0)
                load(1, 1)
                with sp.Fori(0, N // 2 - 1) as r:
                    for u in range(2):
                        step(r * 2 + u, r, u)
                for u in range(2):
                    step(N - 2 + u, N // 2 - 1, u, more=False)
                for u in range(2):
                    sp.wait_ge(stored[u], 16 * (N // 2))

            @block.tensor
            def _(pe):
                def transposes(s, r, u):
                    pe.wait_ge(loaded[u], 64 * (r + 1))
                    wait(pe, xT_copied, s)
                    for side in range(2):
                        for k in range(KC):
                            m = nc.tensor.transpose(psum[:, 0, (2 * side + k) * P:(2 * side + k + 1) * P],
                                                    x_in[:, u, side, k * P:(k + 1) * P], chip.ident[:])
                    m.then_inc(transposed, 1)

                def step(s, r, u):
                    pe.wait_ge(xT_copied, s + 1)
                    wait(pe, qk_copied, s)
                    for side, w, at in ((1, wq_sb, 0), (0, wk_sb, 2)):
                        for t in range(2):
                            for k in range(KC):
                                m = nc.tensor.matmul(psum[:, 1, (at + t) * P:(at + t + 1) * P],
                                                     w[:, k, t * P:(t + 1) * P], xT[:, side, k, :],
                                                     start=(k == 0), stop=(k == KC - 1))
                    m.then_inc(qk_done, 1)
                    wait(pe, v_copied, s)
                    for k in range(KC):
                        m = nc.tensor.matmul(psum[:, 2, 0:C], xT[:, 1, k, :], wv_sb[:, k, :],
                                             start=(k == 0), stop=(k == KC - 1))
                    m.then_inc(v_done, 1)
                    if not (isinstance(s, int) and s == N - 1):
                        transposes(s + 1, r + u, 1 - u)
                    pe.wait_ge(qk_copied, s + 1)
                    wait(pe, scores_copied, s)
                    for t in range(2):
                        for g in range(4):
                            for b in range(B):
                                head, toks = slice(32 * g, 32 * g + 32), slice(b * N, (b + 1) * N)
                                m = nc.tensor.matmul(psum[toks, 3 + g, t * N:(t + 1) * N],
                                                     qk[head, t, toks], qk[head, 2 + t, toks],
                                                     start=True, stop=True)
                    m.then_inc(scores_done, 1)

                pe.wait_ge(weights, 48)
                transposes(0, 0, 0)
                turns(pe, N, step)

            @block.scalar
            def _(act):
                def x_copy(s):
                    act.wait_ge(transposed, s + 1)
                    wait(act, v_done, s)
                    nc.scalar.activation(xT[:].rearrange("p a k n -> p (a k n)"), psum[:, 0, :],
                                         ACT.Copy).then_inc(xT_copied, 1)

                def step(s, r, u):
                    act.wait_ge(v_done, s + 1)
                    wait(act, stored[u], r * 16)
                    nc.scalar.activation(v_out[:, u, :], psum[:, 2, 0:C], ACT.Copy).then_inc(v_copied, 1)
                    if not (isinstance(s, int) and s == N - 1):
                        x_copy(s + 1)
                    act.wait_ge(scores_done, s + 1)
                    nc.scalar.activation(S[:, s, :].rearrange("p (g n) -> p g n", g=4), psum[:, 3:7, 0:P],
                                         ACT.Copy).then_inc(scores_copied, 1)

                x_copy(0)
                turns(act, N, step)

            @block.vector
            def _(dve):
                def step(s, r, u):
                    dve.wait_ge(qk_done, s + 1)
                    wait(dve, scores_done, s)
                    nc.vector.tensor_copy(qk[:].rearrange("p a n -> p (a n)"), psum[:, 1, :]).then_inc(qk_copied, 1)
                    dve.wait_ge(scores_copied, s + 1)
                    if isinstance(s, int) and s == 0:
                        nc.vector.tensor_copy(top[:], S[:, 0, :]).then_inc(maxed, 1)
                    else:
                        dve.wait_ge(maxed, s)
                        nc.vector.tensor_tensor(top[:], top[:], S[:, s, :], ALU.max).then_inc(maxed, 1)

                turns(dve, N, step)

        chip.part = "softmax0"
        shifted, raised, summed, e_stored = (chip.sem(n) for n in ("shifted", "raised", "summed", "e_stored"))
        CH = 4
        JN = N // CH
        with nc.Block() as block:
            @block.vector
            def _(dve):
                def sums(c):
                    dve.wait_ge(raised, c + 1)
                    nc.vector.tensor_reduce(part_sum[:, c, :], S[:, c * JN:(c + 1) * JN, :].rearrange("p j n -> p n j"),
                                            AX.X, ALU.add).then_inc(summed, 1)

                for c in range(CH):
                    piece = S[:, c * JN:(c + 1) * JN, :]
                    nc.vector.tensor_tensor(piece, piece, top[:, None, :].broadcast_to([P, JN, BANK]),
                                            ALU.subtract).then_inc(shifted, 1)
                    if c >= 1:
                        sums(c - 1)
                sums(CH - 1)
                dve.wait_ge(summed, CH)
                nc.vector.tensor_reduce(denom[:], part_sum[:].rearrange("p c n -> p n c"), AX.X,
                                        ALU.add).then_inc(summed, 1)
                dve.wait_ge(summed, CH + 1)
                nc.vector.reciprocal(inverse[:], denom[:]).then_inc(summed, 1)

            @block.scalar
            def _(act):
                for c in range(CH):
                    piece = S[:, c * JN:(c + 1) * JN, :].rearrange("p j n -> p (j n)")
                    act.wait_ge(shifted, c + 1)
                    nc.scalar.activation(piece, piece, ACT.Exp, scale=float(DK) ** -0.5).then_inc(raised, 1)

            @block.sync
            def _(sp):
                for c in range(CH):
                    sp.wait_ge(raised, c + 1)
                    for b in range(B):
                        sp.dma_start(e_dram[b, :, c * JN:(c + 1) * JN, :],
                                     S[b * N:(b + 1) * N, c * JN:(c + 1) * JN, :]).then_inc(e_stored, 16)
                sp.wait_ge(summed, CH + 2)
                sp.dma_start(r_dram.rearrange("b i n -> (b i) n"), inverse[:]).then_inc(e_stored, 16)
                sp.wait_ge(e_stored, 16 * (CH * B + 1))


def active(turn, first, last):
    return not isinstance(turn, int) or first <= turn <= last


def triangle_output(nc, chip, x, wv1, wo, w1, b1, w2, b2, g_agg, be_agg, g_out, be_out, w_fg, w_h,
                    v2_dram, e_dram, r_dram, x1_dram, fg_dram, h_dram):
    chip.part = "out0"
    psum = chip.psum
    LC = 8
    NCH = N // LC
    WS = 4
    FG = w_fg[0].shape[1] + w_fg[1].shape[1]
    with ExitStack() as ctx:
        def sb(name, shape, dt=F32):
            return ctx.enter_context(nc.sbuf_tensor(name, shape, dt))

        wv_sb, wo_sb, wh_sb = sb("wv1_sb", [P, KC, C]), sb("wo_sb", [P, KC, C]), sb("wh_sb", [P, KC, C])
        w1_sb, w2_sb, wfg_sb = sb("w1_sb", [P, KC, FF]), sb("w2_sb", [P, KF, C]), sb("wfg_sb", [P, KC, FG])
        b1_sb, eps = sb("b1_sb", [P, KF]), sb("eps", [P, 1])
        norms = {n: sb(n, [P, C]) for n in ("gain1", "shift1", "bias2", "gain2", "shift2")}
        V2 = sb("V2", [P, N, C])
        W = sb("W", [P, WS, LC, C])
        x_in, xT, v1 = sb("x_row", [P, 2, C]), sb("x_rowT", [P, KC, P]), sb("v1", [P, 2, C])
        e_in = sb("e_in", [P, 2, BANK])
        r_in = sb("r_in", [P, 2, B, BANK])
        att = sb("att", [P, 2, B, BANK])
        o = sb("o", [P, 2, BANK])
        OT = sb("OT", [P, 2, 2, B, N])
        res1, res2 = sb("res1", [P, C]), sb("res2", [P, C])
        stat1, stat2 = sb("stat1", [P, 6]), sb("stat2", [P, 6])
        mv1, mv2 = sb("mv1", [P, 2]), sb("mv2", [P, 2])
        sd1, sd2, rs1, rs2 = (sb(n, [P, 1]) for n in ("sd1", "sd2", "rs1", "rs2"))
        hn, hg, h1, h1b = (sb(n, [P, C]) for n in ("hn", "hg", "h1", "h1b"))
        xn, xg, x1 = sb("xn", [P, C]), sb("xg", [P, C]), sb("x1", [P, 2, C])
        h1T, uT, x1T = sb("h1T", [P, KC, P]), sb("uT", [P, KF, P]), sb("x1T", [P, KC, P])
        fg_out, h_out = sb("fg_out", [FG, 2, P]), sb("h_out", [P, 2, C])

        weights, v2_loaded = chip.sem("weights"), chip.sem("v2_loaded")
        loaded = [chip.sem(f"loaded{u}") for u in range(2)]
        x1_stored = [chip.sem(f"x1_stored{u}") for u in range(2)]
        fgh_stored = [chip.sem(f"fgh_stored{u}") for u in range(2)]
        (cleared, transposed, xT_copied, v1_done, v1_copied, att_ready, w_done, pv_done, o_copied, o_transposed,
         o_spread, attn_done, attn_read, stats1, root1, norm1, h1_steps, h1_transposed, h1T_copied,
         up_done, relu_done, ffn_done, ffn_read, stats2, root2, norm2, x1_steps, x1_transposed, x1T_copied,
         fg_done, fg_copied, h_done, h_copied) = (chip.sem(n) for n in (
             "cleared transposed xT_copied v1_done v1_copied att_ready w_done pv_done o_copied o_transposed "
             "o_spread attn_done attn_read stats1 root1 norm1 h1_steps h1_transposed h1T_copied "
             "up_done relu_done ffn_done ffn_read stats2 root2 norm2 x1_steps x1_transposed x1T_copied "
             "fg_done fg_copied h_done h_copied").split())

        def all_turns(eng, step):
            turns(eng, N + 2, step, head=1, tail=2)

        def slot_after(r, u):
            return 1 - u, r + u

        def slot_before(r, u):
            return 1 - u, r - 1 + u

        with nc.Block() as block:
            @block.sync
            def _(sp):
                def load(i, u):
                    for b in range(B):
                        half = slice(b * N, (b + 1) * N)
                        sp.dma_start(x_in[half, u, :], x[b, i]).then_inc(loaded[u], 16)
                        sp.dma_start(e_in[half, u, :], e_dram[b, i]).then_inc(loaded[u], 16)
                        sp.dma_start(r_in[half, u, b, :], r_dram[b, i][None, :].broadcast_to([N, BANK])).then_inc(loaded[u], 16)

                def step(i, r, u):
                    if active(i, 0, N - 2):
                        wait(sp, transposed, i)
                        wait(sp, att_ready, i)
                        wait(sp, attn_read, i)
                        load(i + 1, 1 - u)
                    if active(i, 2, N + 1):
                        z = i - 2
                        sp.wait_ge(fg_copied, z + 1)
                        sp.wait_ge(h_copied, z + 1)
                        for b in range(B):
                            half = slice(b * N, (b + 1) * N)
                            sp.dma_start(fg_dram[:, b, z, :], fg_out[:, u, half]).then_inc(fgh_stored[u], 16)
                            sp.dma_start(h_dram[b, z], h_out[half, u, :]).then_inc(fgh_stored[u], 16)
                    if active(i, 1, N):
                        m, (v, _) = i - 1, slot_before(r, u)
                        sp.wait_ge(x1_steps, 2 * m + 2)
                        for b in range(B):
                            half = slice(b * N, (b + 1) * N)
                            sp.dma_start(x1_dram[b, m], x1[half, v, :]).then_inc(x1_stored[v], 16)

                sp.wait_ge(cleared, 2)
                load(0, 0)
                for w, dst in ((wv1, wv_sb), (wo, wo_sb), (w1, w1_sb), (w2, w2_sb), (w_h, wh_sb)):
                    sp.dma_start(dst[:], rows(w)).then_inc(weights, 16)
                at = 0
                for w in w_fg:
                    sp.dma_start(wfg_sb[:, :, at:at + w.shape[1]], rows(w)).then_inc(weights, 16)
                    at += w.shape[1]
                with nc.allow_non_contiguous_dma(reason="a bias of 512 words, once"):
                    sp.dma_start(b1_sb[:], b1.rearrange("(k p) -> p k", p=P)).then_inc(weights, 16)
                for name, v in (("gain1", g_agg), ("shift1", be_agg), ("bias2", b2), ("gain2", g_out), ("shift2", be_out)):
                    sp.dma_start(norms[name][:], across(v)).then_inc(weights, 16)
                all_turns(sp, step)
                for u in range(2):
                    sp.wait_ge(x1_stored[u], 16 * B * (N // 2))
                    sp.wait_ge(fgh_stored[u], 32 * B * (N // 2))

            @block.tensor
            def _(pe):
                def x_to_v1(i, r, u, part):
                    if part == 0:
                        pe.wait_ge(loaded[u], 16 * 6 * (r + 1))
                        for k in range(KC):
                            m_ = nc.tensor.transpose(psum[:, 0, k * P:(k + 1) * P], x_in[:, u, k * P:(k + 1) * P],
                                                     chip.ident[:])
                        m_.then_inc(transposed, 1)
                    else:
                        pe.wait_ge(xT_copied, i + 1)
                        wait(pe, fg_copied, i - 2)
                        for k in range(KC):
                            m_ = nc.tensor.matmul(psum[:, 1, 0:C], xT[:, k, :], wv_sb[:, k, :],
                                                  start=(k == 0), stop=(k == KC - 1))
                        m_.then_inc(v1_done, 1)

                def products(i, r, u, c):
                    n = i * NCH + c
                    if c == 0:
                        pe.wait_ge(att_ready, i + 1)
                    pe.wait_ge(w_done, n + 1)
                    wait(pe, o_copied, n - 1)
                    for l in range(LC):
                        q, g = l % 4, l // 4
                        m_ = nc.tensor.matmul(psum[32 * q:32 * q + B * HEADS, 3 + c % 2, g * C:(g + 1) * C],
                                              att[:, u, :, :].rearrange("p b (h l) -> p (b h) l", l=N)[:, :, c * LC + l],
                                              W[:, c % WS, l, :], start=True, stop=True)
                    m_.then_inc(pv_done, 1)

                def turn_around(n, c):
                    pe.wait_ge(o_copied, n + 1)
                    wait(pe, o_spread, n - 1)
                    for g in range(2):
                        for t in range(2):
                            m_ = nc.tensor.transpose(psum[:, 5 + c % 2, (2 * t + g) * P:(2 * t + g + 1) * P],
                                                     o[:, c % 2, (2 * g + t) * P:(2 * g + t + 1) * P], chip.ident[:])
                    m_.then_inc(o_transposed, 1)

                def step(i, r, u):
                    m, z = i - 1, i - 2
                    v, _ = slot_before(r, u)
                    if active(i, 2, N + 1):
                        pe.wait_ge(x1_steps, 2 * z + 2)
                        for k in range(KC):
                            m_ = nc.tensor.transpose(psum[:, 0, k * P:(k + 1) * P], x1[:, u, k * P:(k + 1) * P],
                                                     chip.ident[:])
                        m_.then_inc(x1_transposed, 1)
                    for c in range(NCH):
                        if active(i, 0, N - 1):
                            products(i, r, u, c)
                        if (c > 0 and active(i, 0, N - 1)) or (c == 0 and active(i, 1, N)):
                            turn_around(i * NCH + c - 1, (c - 1) % NCH)
                        if c == 1 and active(i, 1, N):
                            pe.wait_ge(o_spread, i * NCH)
                            wait(pe, ffn_read, m)
                            for k in range(KC):
                                m_ = nc.tensor.matmul(psum[:, 2, 0:C], OT[:, v, k].rearrange("p b l -> p (b l)"),
                                                      wo_sb[:, k, :], start=(k == 0), stop=(k == KC - 1))
                            m_.then_inc(attn_done, 1)
                        if c == 1 and active(i, 2, N + 1):
                            pe.wait_ge(x1T_copied, z + 1)
                            for k in range(KC):
                                m_ = nc.tensor.matmul(psum[0:FG, 1, 0:P], wfg_sb[:, k, :], x1T[:, k, :],
                                                      start=(k == 0), stop=(k == KC - 1))
                            m_.then_inc(fg_done, 1)
                            for k in range(KC):
                                m_ = nc.tensor.matmul(psum[:, 7, 0:C], x1T[:, k, :], wh_sb[:, k, :],
                                                      start=(k == 0), stop=(k == KC - 1))
                            m_.then_inc(h_done, 1)
                        if c == 3 and active(i, 1, N):
                            pe.wait_ge(h1_steps, 3 * m + 2)
                            for k in range(KC):
                                m_ = nc.tensor.transpose(psum[:, 0, k * P:(k + 1) * P], h1[:, k * P:(k + 1) * P],
                                                         chip.ident[:])
                            m_.then_inc(h1_transposed, 1)
                        if c == 4 and active(i, 1, N):
                            pe.wait_ge(h1T_copied, m + 1)
                            wait(pe, h_copied, z + 1)
                            for f in range(KF):
                                for k in range(KC):
                                    m_ = nc.tensor.matmul(psum[:, 7, f * P:(f + 1) * P], w1_sb[:, k, f * P:(f + 1) * P],
                                                          h1T[:, k, :], start=(k == 0), stop=(k == KC - 1))
                            m_.then_inc(up_done, 1)
                        if c == 5 and active(i, 1, N):
                            pe.wait_ge(relu_done, m + 1)
                            for f in range(KF):
                                m_ = nc.tensor.matmul(psum[:, 2, 0:C], uT[:, f, :], w2_sb[:, f, :],
                                                      start=(f == 0), stop=(f == KF - 1))
                            m_.then_inc(ffn_done, 1)
                        if c in (5, 6) and active(i, 0, N - 2):
                            nu, nr = slot_after(r, u)
                            x_to_v1(i + 1, nr, nu, c - 5)

                pe.wait_ge(weights, 16 * 13)
                x_to_v1(0, 0, 0, 0)
                x_to_v1(0, 0, 0, 1)
                all_turns(pe, step)

            @block.scalar
            def _(act):
                def x_copy(i):
                    act.wait_ge(transposed, i + 1)
                    wait(act, v1_done, i)
                    nc.scalar.activation(xT[:], psum[:, 0, 0:C].rearrange("p (k n) -> p k n", k=KC),
                                         ACT.Copy).then_inc(xT_copied, 1)

                def v1_copy(i, u):
                    act.wait_ge(v1_done, i + 1)
                    wait(act, w_done, (i - 1) * NCH)
                    nc.scalar.activation(v1[:, u, :], psum[:, 1, 0:C], ACT.Copy).then_inc(v1_copied, 1)

                def spread(n, c, i, u):
                    act.wait_ge(o_transposed, n + 1)
                    if c == 0:
                        wait(act, attn_done, i - 1)
                    for g in range(4):
                        rows_ = slice(32 * g, 32 * g + 32)
                        base = psum[rows_, 5 + c % 2, 2 * g:2 * g + 1]
                        own = bass.AP(base.tensor, base.offset, [base.ap[0], [257, 2], [8, B], [32, LC]])
                        m_ = nc.scalar.activation(OT[rows_, u, :, :, c * LC:(c + 1) * LC], own, ACT.Copy)
                    m_.then_inc(o_spread, 1)

                def root(var, sd, ready, count, done):
                    act.wait_ge(ready, count)
                    nc.scalar.activation(sd[:], var, ACT.Sqrt, bias=eps[:]).then_inc(done, 1)

                def step(i, r, u):
                    m, z = i - 1, i - 2
                    v, _ = slot_before(r, u)
                    for c in range(NCH):
                        n = i * NCH + c
                        if active(i, 0, N - 1):
                            act.wait_ge(pv_done, n + 1)
                            wait(act, o_transposed, n - 1)
                            nc.scalar.activation(o[:, c % 2, :], psum[:, 3 + c % 2, :], ACT.Copy).then_inc(o_copied, 1)
                        if c > 0 and active(i, 0, N - 1):
                            spread(n - 1, c - 1, i, u)
                        if c == 0 and active(i, 1, N):
                            spread(n - 1, NCH - 1, i - 1, v)
                        if c == 0 and active(i, 2, N + 1):
                            act.wait_ge(x1_transposed, z + 1)
                            wait(act, h_done, z)
                            nc.scalar.activation(x1T[:], psum[:, 0, 0:C].rearrange("p (k n) -> p k n", k=KC),
                                                 ACT.Copy).then_inc(x1T_copied, 1)
                        if c == 1 and active(i, 2, N + 1):
                            act.wait_ge(fg_done, z + 1)
                            wait(act, fgh_stored[u], 32 * B * (r - 1))
                            nc.scalar.activation(fg_out[:, u, :], psum[0:FG, 1, 0:P], ACT.Copy).then_inc(fg_copied, 1)
                            act.wait_ge(h_done, z + 1)
                            nc.scalar.activation(h_out[:, u, :], psum[:, 7, 0:C], ACT.Copy).then_inc(h_copied, 1)
                        if c == 2 and active(i, 1, N):
                            root(mv1[:, 1:2], sd1, stats1, 3 * m + 2, root1)
                        if c == 3 and active(i, 1, N):
                            act.wait_ge(h1_transposed, m + 1)
                            nc.scalar.activation(h1T[:], psum[:, 0, 0:C].rearrange("p (k n) -> p k n", k=KC),
                                                 ACT.Copy).then_inc(h1T_copied, 1)
                        if c == 4 and active(i, 1, N):
                            act.wait_ge(up_done, m + 1)
                            wait(act, ffn_done, m)
                            for f in range(KF):
                                m_ = nc.scalar.activation(uT[:, f, :], psum[:, 7, f * P:(f + 1) * P], ACT.Relu,
                                                          bias=b1_sb[:, f:f + 1])
                            m_.then_inc(relu_done, 1)
                        if c == 5 and active(i, 0, N - 2):
                            x_copy(i + 1)
                        if c == 6 and active(i, 0, N - 2):
                            v1_copy(i + 1, 1 - u)
                        if c == 6 and active(i, 1, N):
                            root(mv2[:, 1:2], sd2, stats2, 3 * m + 2, root2)

                act.wait_ge(cleared, 2)
                act.wait_ge(weights, 16 * 13)
                x_copy(0)
                v1_copy(0, 0)
                all_turns(act, step)

            @block.vector
            def _(dve):
                def step(i, r, u):
                    m = i - 1
                    v, _ = slot_before(r, u)
                    for c in range(NCH):
                        n = i * NCH + c
                        if active(i, 0, N - 1):
                            if c == 0:
                                dve.wait_ge(v1_copied, i + 1)
                            wait(dve, pv_done, n - WS + 1)
                            nc.vector.tensor_tensor(W[:, c % WS], V2[:, c * LC:(c + 1) * LC, :],
                                                    v1[:, u, None, :].broadcast_to([P, LC, C]),
                                                    ALU.mult).then_inc(w_done, 1)
                        if c == 1 and active(i, 1, N):
                            dve.wait_ge(attn_done, m + 1)
                            nc.vector.tensor_tensor(res1[:], psum[:, 2, 0:C], x_in[:, v, :],
                                                    ALU.add).then_inc(attn_read, 1)
                            dve.wait_ge(attn_read, m + 1)
                            nc.vector.bn_stats(stat1[:], res1[:]).then_inc(stats1, 1)
                            dve.drain()
                            nc.vector.bn_aggr(mv1[:], stat1[:]).then_inc(stats1, 1)
                        if c == 2 and active(i, 1, N):
                            dve.wait_ge(root1, m + 1)
                            nc.vector.reciprocal(rs1[:], sd1[:]).then_inc(stats1, 1)
                            dve.wait_ge(stats1, 3 * m + 3)
                            wait(dve, h1_steps, 3 * m)
                            nc.vector.tensor_scalar(hn[:], res1[:], mv1[:, 0:1], rs1[:], ALU.subtract,
                                                    ALU.mult).then_inc(norm1, 1)
                        if c == 5 and active(i, 1, N):
                            dve.wait_ge(ffn_done, m + 1)
                            dve.wait_ge(h1_steps, 3 * m + 3)
                            nc.vector.tensor_tensor(res2[:], psum[:, 2, 0:C], h1b[:], ALU.add).then_inc(ffn_read, 1)
                            dve.wait_ge(ffn_read, m + 1)
                            nc.vector.bn_stats(stat2[:], res2[:]).then_inc(stats2, 1)
                            dve.drain()
                            nc.vector.bn_aggr(mv2[:], stat2[:]).then_inc(stats2, 1)
                        if c == 6 and active(i, 1, N):
                            dve.wait_ge(root2, m + 1)
                            nc.vector.reciprocal(rs2[:], sd2[:]).then_inc(stats2, 1)
                            dve.wait_ge(stats2, 3 * m + 3)
                            wait(dve, x1_steps, 2 * m)
                            nc.vector.tensor_scalar(xn[:], res2[:], mv2[:, 0:1], rs2[:], ALU.subtract,
                                                    ALU.mult).then_inc(norm2, 1)

                nc.vector.memset(eps[:], 1e-5).then_inc(cleared, 1)
                nc.vector.memset(r_in[:], 0.0).then_inc(cleared, 1)
                dve.wait_ge(weights, 16 * 13)
                dve.wait_ge(v2_loaded, 16 * 4)
                all_turns(dve, step)

            @block.gpsimd
            def _(pool):
                def attention(i, r, u):
                    pool.wait_ge(loaded[u], 16 * 6 * (r + 1))
                    wait(pool, pv_done, (i - 1) * NCH)
                    nc.gpsimd.tensor_tensor(att[:, u], e_in[:, u, None, :].broadcast_to([P, B, BANK]), r_in[:, u],
                                            ALU.mult).then_inc(att_ready, 1)

                def step(i, r, u):
                    m = i - 1
                    v, vr = slot_before(r, u)
                    if active(i, 1, N):
                        pool.wait_ge(norm1, m + 1)
                        wait(pool, h1_steps, 3 * m)
                        nc.gpsimd.tensor_tensor(hg[:], hn[:], norms["gain1"][:], ALU.mult).then_inc(h1_steps, 1)
                        pool.wait_ge(h1_steps, 3 * m + 1)
                        wait(pool, h1_transposed, m)
                        nc.gpsimd.tensor_tensor(h1[:], hg[:], norms["shift1"][:], ALU.add).then_inc(h1_steps, 1)
                        pool.wait_ge(h1_steps, 3 * m + 2)
                        wait(pool, ffn_read, m)
                        nc.gpsimd.tensor_tensor(h1b[:], h1[:], norms["bias2"][:], ALU.add).then_inc(h1_steps, 1)
                    if active(i, 0, N - 2):
                        nu, nr = slot_after(r, u)
                        attention(i + 1, nr, nu)
                    if active(i, 1, N):
                        pool.wait_ge(norm2, m + 1)
                        nc.gpsimd.tensor_tensor(xg[:], xn[:], norms["gain2"][:], ALU.mult).then_inc(x1_steps, 1)
                        pool.wait_ge(x1_steps, 2 * m + 1)
                        wait(pool, x1_transposed, m - 1)
                        wait(pool, x1_stored[v], 16 * B * vr)
                        nc.gpsimd.tensor_tensor(x1[:, v, :], xg[:], norms["shift2"][:], ALU.add).then_inc(x1_steps, 1)

                for piece in range(4):
                    ls = slice(piece * N // 4, (piece + 1) * N // 4)
                    pool.dma_start(V2[:, ls, :], v2_dram[ls].rearrange("l p c -> p l c")).then_inc(v2_loaded, 16)
                pool.wait_ge(weights, 16 * 13)
                attention(0, 0, 0)
                all_turns(pool, step)


QT = 512
NT = HW // QT
SUB = QT // P
MT = HW // P
MC = HW // BANK
D = 32
RING = 4


def attention(nc, chip, name, k_dram, q_dram, v_dram, x_dram, scale, gamma, channel, load_first, store):
    chip.part = name
    psum = chip.psum
    MAXU = SUB * MC
    units = ["max"] * MAXU + ["turn"] * 2 + (["channel"] * SUB if channel else [])
    NU = len(units)
    SPAN = 25
    unit_at = [[] for _ in range(MT)]
    for n in range(MAXU):
        unit_at[2 + n * SPAN // MAXU].append(n)
    for n in range(MAXU, NU):
        unit_at[SPAN + 4].append(n)
    with ExitStack() as ctx:
        def sb(tag, shape, dt=F32):
            return ctx.enter_context(nc.sbuf_tensor(f"{name}_{tag}", shape, dt))

        k_raw, v_raw = sb("k_raw", [D, HW]), sb("v_raw", [P, MT, C])
        K = sb("K", [3 * D + 2, HW], F32R)
        Q = sb("Q", [3 * D + 2, 2, QT], F32R)
        V_hi, V_lo = sb("V_hi", [P, MT, C + 2], F32R), sb("V_lo", [P, MT, C], F32R)
        q_raw, x_in = sb("q_raw", [D, 2, QT]), sb("x_in", [P, 2, SUB, C])
        e, e_hi, e_lo = sb("e", [P, RING, QT]), sb("e_hi", [P, RING, QT], F32R), sb("e_lo", [P, RING, QT], F32R)
        tops, top, minus = sb("tops", [P, SUB, MC]), sb("top", [P, SUB]), sb("minus", [P, SUB, 1])
        minus2 = sb("minus2", [P, SUB, 2], F32R)
        inv, inv_g, gam = sb("inv", [P, SUB]), sb("inv_g", [P, SUB]), sb("gam", [P, 1])
        y = sb("y", [P, 2, SUB, C])
        if channel:
            cvT, mix, batch_mix = sb("cvT", [D, 2, QT]), sb("mix", [D, B, C]), sb("batch_mix", [D, C])

        set_up, first_loaded = chip.sem("set_up"), chip.sem("first_loaded")
        kv_loaded, kv_hi, kv_ready = chip.sem("kv_loaded"), chip.sem("kv_hi"), chip.sem("kv_ready")
        loaded = [chip.sem(f"loaded{u}") for u in range(2)]
        stored = [chip.sem(f"stored{u}") for u in range(2)]
        q_hi, q_ready = chip.sem("q_hi"), chip.sem("q_ready")
        unit_done, unit_free, chained, max_ready = (chip.sem(n) for n in ("unit_done", "unit_free", "chained", "max_ready"))
        scored, raised, split, probs_free = (chip.sem(n) for n in ("scored", "raised", "split", "probs_free"))
        passed = chip.sem("passed")
        inverted, y_done = chip.sem("inverted"), chip.sem("y_done")
        LOADS = 3 if channel else 2
        STORES = store.count

        def tiles(eng, b, step):
            with eng.Fori(0, NT // 2 - 1) as r:
                for u in range(2):
                    step(b * NT + r * 2 + u, r * 2 + u, b * (NT // 2) + r, u, False)
            for u in range(2):
                t = NT - 2 + u
                step(b * NT + t, t, b * (NT // 2) + (NT // 2 - 1), u, u == 1)

        with nc.Block() as block:
            @block.sync
            def _(sp):
                def load(b, t, u):
                    sp.dma_start(q_raw[:, u, :], q_dram[:, b, bass.ds(t * QT, QT)]).then_inc(loaded[u], 16)
                    sp.dma_start(x_in[:, u], x_dram[b, bass.ds(t * QT, QT), :].rearrange("(j p) c -> p j c", p=P)).then_inc(loaded[u], 16)
                    if channel:
                        sp.dma_start(cvT[:, u, :], channel[:, b, bass.ds(t * QT, QT)]).then_inc(loaded[u], 16)

                load_first(sp, gam, mix if channel else None, first_loaded)
                with sp.Fori(0, B) as b:
                    sp.wait_ge(kv_ready, b * 2)
                    sp.dma_start(k_raw[:], k_dram[:, b, :]).then_inc(kv_loaded, 16)
                    sp.dma_start(v_raw[:], v_dram[b].rearrange("(m p) c -> p m c", p=P)).then_inc(kv_loaded, 16)
                    sp.wait_ge(y_done, b * (NT * SUB))
                    sp.sem_inc(passed, 1)
                    load(b, 0, 0)

                    def step(tt, t, rr, u, last):
                        sp.wait_ge(y_done, tt * SUB)
                        sp.sem_inc(passed, 1)
                        if not last:
                            load(b, t + 1, 1 - u)
                        sp.wait_ge(y_done, (tt + 1) * SUB)
                        sp.sem_inc(passed, 1)
                        store(sp, b, t, y[:, u], stored[u])

                    tiles(sp, b, step)
                for u in range(2):
                    sp.wait_ge(stored[u], 16 * STORES * (B * NT // 2))

            @block.tensor
            def _(pe):
                def unit(n, tt, u, rr):
                    pe.wait_ge(unit_free, tt * NU + n + 1)
                    bank = 6 + n % 2
                    if units[n] == "max":
                        j, c = n // MC, n % MC
                        m = nc.tensor.matmul(psum[:, bank, :], Q[0:3 * D, u, j * P:(j + 1) * P],
                                             K[0:3 * D, c * BANK:(c + 1) * BANK], start=True, stop=True)
                    elif units[n] == "turn":
                        if n == MAXU:
                            pe.wait_ge(chained, (tt + 1) * 4)
                        for j in (0, 1):
                            jj = 2 * (n - MAXU) + j
                            m = nc.tensor.transpose(psum[0:2, bank, j * P:(j + 1) * P],
                                                    minus2[:, jj, :].bitcast(F32), chip.ident[:])
                    else:
                        j = n - MAXU - 2
                        if j == 0:
                            pe.wait_ge(loaded[u], 16 * LOADS * (rr + 1))
                        m = nc.tensor.matmul(psum[:, bank, 0:C], cvT[:, u, j * P:(j + 1) * P],
                                             batch_mix[:], start=True, stop=True)
                    m.then_inc(unit_done, 1)

                def scores(k, u):
                    nc.tensor.matmul(psum[:, 4 + k % 2, :], K[:, k * P:(k + 1) * P], Q[:, u, :],
                                     start=True, stop=True).then_inc(scored, 1)

                def step(tt, t, rr, u, last):
                    for k in range(MT):
                        n = tt * MT + k
                        if k < MT - 1 or not last:
                            if k == MT - 1:
                                pe.wait_ge(max_ready, tt + 2)
                            pe.wait_ge(raised, n)
                            scores((k + 1) % MT, u if k < MT - 1 else 1 - u)
                        if not last:
                            if k == 2:
                                pe.wait_ge(q_ready, tt + 2)
                            for w in unit_at[k]:
                                unit(w, tt + 1, 1 - u, rr + u)
                        pe.wait_ge(split, n + 1)
                        for j in range(SUB):
                            part = slice(j * P, (j + 1) * P)
                            if k == 0:
                                pe.wait_ge(y_done, tt * SUB)
                            first, final = k == 0, k == MT - 1
                            nc.tensor.matmul(psum[:, j, 0:C + 2], e_hi[:, k % RING, part], V_hi[:, k, :],
                                             start=first, stop=False)
                            nc.tensor.matmul(psum[:, j, 0:C], e_hi[:, k % RING, part], V_lo[:, k, :],
                                             start=False, stop=False)
                            m = nc.tensor.matmul(psum[:, j, 0:C + 2], e_lo[:, k % RING, part], V_hi[:, k, :],
                                                 start=False, stop=final)
                        m.then_inc(probs_free, 1)

                pe.sem_inc(probs_free, RING)
                pe.wait_ge(set_up, 5)
                with pe.Fori(0, B) as b:
                    pe.wait_ge(kv_ready, b * 2 + 2)
                    pe.wait_ge(q_ready, b * NT + 1)
                    for w in range(NU):
                        unit(w, b * NT, 0, b * (NT // 2))
                    pe.wait_ge(max_ready, b * NT + 1)
                    pe.wait_ge(raised, b * (NT * MT))
                    scores(0, 0)
                    tiles(pe, b, step)

            @block.scalar
            def _(act):
                def q_parts(tt, rr, u):
                    act.wait_ge(loaded[u], 16 * LOADS * (rr + 1))
                    for at in (0, D):
                        nc.scalar.activation(Q[at:at + D, u, :], q_raw[:, u, :], ACT.Copy).then_inc(q_hi, 1)

                def step(tt, t, rr, u, last):
                    for k in range(MT):
                        n = tt * MT + k
                        if k == 1 and not last:
                            act.wait_ge(scored, tt * MT)
                            q_parts(tt + 1, rr + u, 1 - u)
                        act.wait_ge(scored, n + 1)
                        act.wait_ge(probs_free, n + 1)
                        nc.scalar.activation(e[:, k % RING, :], psum[:, 4 + k % 2, :], ACT.Exp, scale=scale)
                        nc.scalar.activation(e_hi[:, k % RING, :], psum[:, 4 + k % 2, :], ACT.Exp,
                                             scale=scale).then_inc(raised, 1)

                with act.Fori(0, B) as b:
                    act.wait_ge(kv_loaded, b * 32 + 32)
                    act.wait_ge(scored, b * (NT * MT))
                    for at in (0, 2 * D):
                        nc.scalar.activation(K[at:at + D, :], k_raw[:], ACT.Copy).then_inc(kv_hi, 1)
                    act.wait_ge(probs_free, b * (NT * MT) + RING)
                    nc.scalar.activation(V_hi[:, :, 0:C], v_raw[:], ACT.Copy).then_inc(kv_hi, 1)
                    q_parts(b * NT, b * (NT // 2), 0)
                    tiles(act, b, step)

            @block.vector
            def _(dve):
                def q_low(tt, u):
                    dve.wait_ge(q_hi, 2 * tt + 2)
                    nc.vector.tensor_tensor(Q[2 * D:3 * D, u, :], q_raw[:, u, :], Q[0:D, u, :].bitcast(F32),
                                            ALU.subtract).then_inc(q_ready, 1)

                def unit(n, tt, u, rr):
                    bank = 6 + n % 2
                    if units[n] == "max":
                        dve.wait_ge(unit_done, tt * NU + n + 1)
                        if n == 0:
                            dve.wait_ge(chained, tt * 4)
                        j, c = n // MC, n % MC
                        nc.vector.tensor_reduce(tops[:, j, c:c + 1], psum[:, bank, :], AX.X, ALU.max).then_inc(unit_free, 1)
                        if n == MAXU - 1:
                            dve.wait_ge(unit_free, tt * NU + 2 + MAXU)
                            nc.vector.tensor_reduce(top[:], tops[:], AX.X, ALU.max).then_inc(chained, 1)
                            dve.wait_ge(chained, tt * 4 + 1)
                            nc.vector.tensor_scalar(minus[:, :, 0], top[:], -1.0, None, ALU.mult).then_inc(chained, 1)
                            dve.wait_ge(chained, tt * 4 + 2)
                            nc.vector.tensor_copy(minus2[:, :, 0:1], minus[:]).then_inc(chained, 1)
                            dve.wait_ge(chained, tt * 4 + 3)
                            nc.vector.tensor_tensor(minus2[:, :, 1:2], minus[:], minus2[:, :, 0:1].bitcast(F32),
                                                    ALU.subtract).then_inc(chained, 1)
                    elif units[n] == "turn":
                        h = n - MAXU
                        dve.wait_ge(unit_done, tt * NU + n + 1)
                        nc.vector.tensor_copy(Q[3 * D:3 * D + 2, u, h * 2 * P:(h + 1) * 2 * P],
                                              psum[0:2, bank, 0:2 * P]).then_inc(unit_free, 1)
                        if h == 1:
                            dve.wait_ge(unit_free, tt * NU + 2 + n + 1)
                            nc.vector.tensor_copy(top[0:1, 0:1], top[0:1, 1:2]).then_inc(max_ready, 1)
                    else:
                        j = n - MAXU - 2
                        if j == 0:
                            dve.wait_ge(loaded[u], 16 * LOADS * (rr + 1))
                        dve.wait_ge(unit_done, tt * NU + n + 1)
                        nc.vector.tensor_tensor(x_in[:, u, j, :], psum[:, bank, 0:C], x_in[:, u, j, :],
                                                ALU.add).then_inc(unit_free, 1)

                def finish(tt, rr, u):
                    dve.wait_ge(probs_free, RING + (tt + 1) * MT)
                    dve.wait_ge(loaded[u], 16 * LOADS * (rr + 1))
                    dve.wait_ge(stored[u], 16 * STORES * rr)
                    nc.vector.reciprocal(inv[:, :, None], psum[:, 0:SUB, C:C + 1]).then_inc(inverted, 1)
                    dve.wait_ge(inverted, 2 * tt + 1)
                    if gamma:
                        nc.vector.tensor_scalar(inv_g[:], inv[:], gam[:], None, ALU.mult).then_inc(inverted, 1)
                    else:
                        nc.vector.tensor_copy(inv_g[:], inv[:]).then_inc(inverted, 1)
                    dve.wait_ge(inverted, 2 * tt + 2)
                    if channel:
                        dve.wait_ge(unit_free, (tt + 1) * NU + 2)
                    for j in range(SUB):
                        nc.vector.scalar_tensor_tensor(out=y[:, u, j, :], in0=psum[:, j, 0:C], scalar=inv_g[:, j:j + 1],
                                                       in1=x_in[:, u, j, :], op0=ALU.mult, op1=ALU.add).then_inc(y_done, 1)

                def step(tt, t, rr, u, last):
                    for k in range(MT):
                        n = tt * MT + k
                        dve.wait_ge(raised, n + 1)
                        dve.wait_ge(probs_free, n + 1)
                        nc.vector.tensor_tensor(e_lo[:, k % RING, :], e[:, k % RING, :],
                                                e_hi[:, k % RING, :].bitcast(F32), ALU.subtract).then_inc(split, 1)
                        if not last:
                            if k == 1:
                                q_low(tt + 1, 1 - u)
                            for w in unit_at[k]:
                                unit(w, tt + 1, 1 - u, rr + u)
                    finish(tt, rr, u)

                nc.vector.memset(K[3 * D:3 * D + 2, :].bitcast(F32), 1.0).then_inc(set_up, 1)
                nc.vector.memset(V_hi[:, :, C:C + 1].bitcast(F32), 1.0).then_inc(set_up, 1)
                nc.vector.memset(V_hi[:, :, C + 1:C + 2].bitcast(F32), 0.0).then_inc(set_up, 1)
                nc.vector.memset(top[:], 0.0).then_inc(set_up, 1)
                dve.wait_ge(first_loaded, 16 * load_first.count)
                nc.vector.sem_inc(unit_free, 2)
                nc.vector.sem_inc(set_up, 1)
                with dve.Fori(0, B) as b:
                    if channel:
                        nc.vector.tensor_copy(batch_mix[:], mix[:, b, :])
                    dve.wait_ge(kv_hi, b * 3 + 2)
                    nc.vector.tensor_tensor(K[D:2 * D, :], k_raw[:], K[0:D, :].bitcast(F32),
                                            ALU.subtract).then_inc(kv_ready, 1)
                    q_low(b * NT, 0)
                    dve.wait_ge(kv_hi, b * 3 + 3)
                    nc.vector.tensor_tensor(V_lo[:], v_raw[:], V_hi[:, :, 0:C].bitcast(F32),
                                            ALU.subtract).then_inc(kv_ready, 1)
                    for w in range(NU):
                        unit(w, b * NT, 0, b * (NT // 2))
                    tiles(dve, b, step)


CR = 16
TILES = T // P
TB = HW // P


def project2(nc, chip, x2_dram, wq, bq, wk, bk, wv, bv, wcq, bcq, wck, bck, wcv, bcv, wp, bp,
             qkc_dram, v_dram, mix_dram):
    chip.part = "project2"
    psum = chip.psum
    CV = C + 2 * CR
    with ExitStack() as ctx:
        def sb(name, shape, dt=F32):
            return ctx.enter_context(nc.sbuf_tensor("p2_" + name, shape, dt))

        w_t, w_m = sb("w_t", [P, KC, 3 * D]), sb("w_m", [P, KC, CV])
        b_t, b_m = sb("b_t", [3 * D, 1]), sb("b_m", [P, CV])
        wp_sb = sb("wp", [CR, C])
        x_in, xT = sb("x_in", [P, 2, C]), sb("xT", [P, 2, KC, P])
        t_out, v_out = sb("t_out", [3 * D, 2, P]), sb("v_out", [P, 2, C])
        cqk = sb("cqk", [P, TILES, 2 * CR])
        top, low, total, inv = (sb(n, [CR, B]) for n in ("top", "low", "total", "inv"))
        ex, attn = sb("ex", [CR, B, CR]), sb("attn", [CR, B, CR])
        mix = sb("mix", [D, B, C])

        cleared, weights, mix_loaded = chip.sem("cleared"), chip.sem("weights"), chip.sem("mix_loaded")
        loaded = [chip.sem(f"loaded{u}") for u in range(2)]
        stored = [chip.sem(f"stored{u}") for u in range(2)]
        transposed, xT_copied, t_done, t_copied, v_done, v_copied = (chip.sem(n) for n in (
            "transposed", "xT_copied", "t_done", "t_copied", "v_done", "v_copied"))
        scored, steps, raised, mixed, mix_stored = (chip.sem(n) for n in ("scored", "steps", "raised", "mixed", "mix_stored"))
        NW = 6 + 6 + 1

        with nc.Block() as block:
            @block.sync
            def _(sp):
                def load(s, u):
                    sp.dma_start(x_in[:, u, :], x2_dram[bass.ds(s * P, P), :]).then_inc(loaded[u], 16)

                def step(s, r, u, more=True):
                    if more:
                        sp.wait_ge(transposed, s + 1)
                        load(s + 2, u)
                    sp.wait_ge(t_copied, s + 1)
                    sp.dma_start(qkc_dram[:, bass.ds(s * P, P)], t_out[:, u, :]).then_inc(stored[u], 16)
                    sp.wait_ge(v_copied, 2 * s + 1)
                    sp.dma_start(v_dram[bass.ds(s * P, P), :], v_out[:, u, :]).then_inc(stored[u], 16)

                load(0, 0)
                load(1, 1)
                sp.wait_ge(cleared, 5)
                for at, w, b in ((0, wq, bq), (D, wk, bk), (2 * D, wcv, bcv)):
                    sp.dma_start(w_t[:, :, at:at + CR], rows(w)).then_inc(weights, 16)
                    sp.dma_start(b_t[at:at + CR, :], column(b)).then_inc(weights, 16)
                for at, w, b in ((0, wv, bv), (C, wcq, bcq), (C + CR, wck, bck)):
                    n = w.shape[1]
                    sp.dma_start(w_m[:, :, at:at + n], rows(w)).then_inc(weights, 16)
                    sp.dma_start(b_m[:, at:at + n], across(b)).then_inc(weights, 16)
                sp.dma_start(wp_sb[:], wp).then_inc(weights, 16)
                for b in range(B):
                    sp.dma_start(mix[CR:CR + 1, b, :], across(bp, 1)).then_inc(mix_loaded, 16)
                with sp.Fori(0, TILES // 2 - 1) as r:
                    for u in range(2):
                        step(r * 2 + u, r, u)
                for u in range(2):
                    step(TILES - 2 + u, TILES // 2 - 1, u, more=False)
                sp.wait_ge(mix_loaded, 16 * B)
                sp.wait_ge(steps, 5)
                sp.dma_start(mix_dram, mix[:]).then_inc(mix_stored, 16)
                for u in range(2):
                    sp.wait_ge(stored[u], 2 * 16 * (TILES // 2))
                sp.wait_ge(mix_stored, 16)

            @block.tensor
            def _(pe):
                def transposes(s, r, u):
                    pe.wait_ge(loaded[u], 16 * (r + 1))
                    wait(pe, xT_copied, s - 1)
                    for k in range(KC):
                        m = nc.tensor.transpose(psum[:, u, k * P:(k + 1) * P], x_in[:, u, k * P:(k + 1) * P],
                                                chip.ident[:])
                    m.then_inc(transposed, 1)

                def step(s, r, u):
                    if not (isinstance(s, int) and s == TILES - 1):
                        transposes(s + 1, r + u, 1 - u)
                    pe.wait_ge(xT_copied, s + 1)
                    wait(pe, t_copied, s - 1)
                    for k in range(KC):
                        m = nc.tensor.matmul(psum[0:3 * D, 2 + u, 0:P], w_t[:, k, :], xT[:, u, k, :],
                                             start=(k == 0), stop=(k == KC - 1))
                    m.then_inc(t_done, 1)
                    wait(pe, v_copied, 2 * (s - 1))
                    for k in range(KC):
                        m = nc.tensor.matmul(psum[:, 4 + u, 0:CV], xT[:, u, k, :], w_m[:, k, :],
                                             start=(k == 0), stop=(k == KC - 1))
                    m.then_inc(v_done, 1)

                pe.wait_ge(weights, 16 * NW)
                transposes(0, 0, 0)
                turns(pe, TILES, step)
                pe.wait_ge(v_copied, 2 * TILES)
                for b in range(B):
                    for s in range(TB):
                        m = nc.tensor.matmul(psum[0:CR, 6, b * CR:(b + 1) * CR], cqk[:, b * TB + s, CR:2 * CR],
                                             cqk[:, b * TB + s, 0:CR], start=(s == 0), stop=(s == TB - 1))
                m.then_inc(scored, 1)
                pe.wait_ge(steps, 4)
                for b in range(B):
                    m = nc.tensor.matmul(psum[0:CR, 7, b * C:(b + 1) * C], attn[:, b, :], wp_sb[:],
                                         start=True, stop=True)
                m.then_inc(mixed, 1)

            @block.scalar
            def _(act):
                def step(s, r, u):
                    act.wait_ge(transposed, s + 1)
                    wait(act, v_done, s - 1)
                    nc.scalar.activation(xT[:, u], psum[:, u, 0:C].rearrange("p (k n) -> p k n", k=KC),
                                         ACT.Copy).then_inc(xT_copied, 1)
                    act.wait_ge(t_done, s + 1)
                    wait(act, stored[u], 2 * 16 * r)
                    nc.scalar.activation(t_out[:, u, :], psum[0:3 * D, 2 + u, 0:P], ACT.Identity,
                                         bias=b_t[:]).then_inc(t_copied, 1)

                act.wait_ge(weights, 16 * NW)
                turns(act, TILES, step)
                act.wait_ge(steps, 2)
                for b in range(B):
                    nc.scalar.activation(ex[:, b, :], psum[0:CR, 6, b * CR:(b + 1) * CR], ACT.Exp, bias=low[:, b:b + 1],
                                         scale=float(CR) ** -0.5, accum_out=total[:, b:b + 1]).then_inc(raised, 1)

            @block.vector
            def _(dve):
                def step(s, r, u):
                    dve.wait_ge(v_done, s + 1)
                    wait(dve, stored[u], 2 * 16 * r)
                    nc.vector.tensor_tensor(v_out[:, u, :], psum[:, 4 + u, 0:C], b_m[:, 0:C], ALU.add).then_inc(v_copied, 1)
                    nc.vector.tensor_tensor(cqk[:, s, :], psum[:, 4 + u, C:CV], b_m[:, C:CV], ALU.add).then_inc(v_copied, 1)

                nc.vector.memset(w_t[:], 0.0).then_inc(cleared, 1)
                nc.vector.memset(b_t[0:2 * D, :], 0.0).then_inc(cleared, 1)
                nc.vector.memset(b_t[2 * D:3 * D, :], 1.0).then_inc(cleared, 1)
                nc.vector.memset(mix[:], 0.0).then_inc(cleared, 1)
                nc.vector.memset(total[:], 0.0).then_inc(cleared, 1)
                dve.wait_ge(weights, 16 * NW)
                turns(dve, TILES, step)
                dve.wait_ge(scored, 1)
                nc.vector.tensor_reduce(top[:], psum[0:CR, 6, 0:B * CR].rearrange("p (b n) -> p b n", b=B),
                                        AX.X, ALU.max).then_inc(steps, 1)
                dve.wait_ge(steps, 1)
                nc.vector.tensor_scalar(low[:], top[:], -float(CR) ** -0.5, None, ALU.mult).then_inc(steps, 1)
                dve.wait_ge(raised, B)
                nc.vector.reciprocal(inv[:], total[:]).then_inc(steps, 1)
                dve.wait_ge(steps, 3)
                nc.vector.tensor_tensor(attn[:], ex[:], inv[:, :, None].broadcast_to([CR, B, CR]), ALU.mult).then_inc(steps, 1)
                dve.wait_ge(mixed, 1)
                nc.vector.tensor_copy(mix[0:CR, :, :], psum[0:CR, 7, :].rearrange("p (b c) -> p b c", b=B)).then_inc(steps, 1)


S1 = N + 1
S2 = N + 2


def clear_borders(nc, chip, corners_dram, padded_dram):
    chip.part = "borders"
    zeros_ready, stored = chip.sem("zeros_ready"), chip.sem("stored")
    with nc.sbuf_tensor("zeros", [S2, 2 * C], F32) as zeros, nc.Block() as block:
        @block.gpsimd
        def _(pool):
            nc.gpsimd.memset(zeros[:], 0.0).then_inc(zeros_ready, 1)

        @block.sync
        def _(sp):
            sp.wait_ge(zeros_ready, 1)
            count = 0
            for b in range(B):
                at = corners_dram[b]
                for dst in (at[0, :, 0:2, :], at[S1 - 1, :, 2:4, :]):
                    sp.dma_start(dst.rearrange("x k c -> x (k c)"), zeros[0:S1, :]).then_inc(stored, 16)
                    count += 1
                for dst in (at[1:S1, 0, 0, :], at[0:S1 - 1, 0, 2, :], at[1:S1, S1 - 1, 1, :], at[0:S1 - 1, S1 - 1, 3, :]):
                    sp.dma_start(dst, zeros[0:N, 0:C]).then_inc(stored, 16)
                    count += 1
                pad = padded_dram[b]
                for dst, n in ((pad[0], S2), (pad[S2 - 1], S2), (pad[1:S2 - 1, 0], N), (pad[1:S2 - 1, S2 - 1], N)):
                    sp.dma_start(dst, zeros[0:n, 0:C]).then_inc(stored, 16)
                    count += 1
            sp.wait_ge(stored, 16 * count)


def corner_store(corners_dram, padded_dram):
    def store(sp, b, t, y_slot, sem):
        for h in range(2):
            half = y_slot[h * N:(h + 1) * N]
            sp.dma_start(padded_dram[b, bass.ds(t * (QT // N) + h + 1, SUB, 2), 1:N + 1, :].rearrange("j x c -> x j c"),
                         half).then_inc(sem, 16)
            for dy in range(2):
                for dx in range(2):
                    sp.dma_start(corners_dram[b, bass.ds(t * (QT // N) + h + 1 - dy, SUB, 2), 1 - dx:N + 1 - dx,
                                              2 * dy + dx, :].rearrange("j x c -> x j c"), half).then_inc(sem, 16)

    store.count = 2 * (1 + 4)
    return store


TAPS = 9
OFF = 3 * TAPS
OQ = 32
GROUPS = P // OQ
YT = 8
YTOK = YT * N
SPAN_ROWS = (YT + 2) * S2
FULL = SPAN_ROWS // P
REST = SPAN_ROWS - FULL * P


def offsets(nc, chip, padded_dram, offset_w, off_all):
    chip.part = "offsets"
    psum = chip.psum
    OT = B * N // YT
    with ExitStack() as ctx:
        def sb(name, shape, dt=F32):
            return ctx.enter_context(nc.sbuf_tensor("off_" + name, shape, dt))

        w = sb("w", [P, TAPS, KC, OQ])
        stack = sb("stack", [P, OQ])
        x_in = sb("x_in", [P, 2, FULL + 1, C])
        xT = sb("xT", [P, 2, KC, SPAN_ROWS])
        oT = sb("oT", [P, 2, YTOK])
        cleared, weights = chip.sem("cleared"), chip.sem("weights")
        loaded = [chip.sem(f"loaded{u}") for u in range(2)]
        turned, xT_copied, xT2_copied, convolved, oT_copied, added, kept = (chip.sem(n) for n in (
            "turned", "xT_copied", "xT2_copied", "convolved", "oT_copied", "added", "kept"))

        with nc.Block() as block:
            @block.sync
            def _(sp):
                def load(b, yt, u):
                    rows_at = padded_dram[b].rearrange("y x c -> (y x) c")
                    sp.dma_start(x_in[:, u, 0:FULL, :], rows_at[bass.ds(yt * (YT * S2), FULL * P), :]
                                 .rearrange("(i p) c -> p i c", p=P)).then_inc(loaded[u], 16)
                    sp.dma_start(x_in[0:REST, u, FULL, :], rows_at[bass.ds(yt * (YT * S2) + FULL * P, REST), :]
                                 ).then_inc(loaded[u], 16)

                sp.wait_ge(cleared, 1)
                sp.dma_start(w[:, :, :, 0:OFF], offset_w.rearrange("a b (k p) f -> p (a b) k f", p=P)).then_inc(weights, 16)
                load(0, 0, 0)
                load(0, 1, 1)
                with sp.Fori(1, OT // 2 // B) as r:
                    for u in range(2):
                        sp.wait_ge(turned, r * 2 + u - 1)
                        load(0, r * 2 + u, u)
                with sp.Fori(0, OT // 2 // B) as r:
                    for u in range(2):
                        sp.wait_ge(turned, r * 2 + u + OT // B - 1)
                        load(1, r * 2 + u, u)

            @block.tensor
            def _(pe):
                def turn(s, r, u):
                    pe.wait_ge(loaded[u], 32 * (r + 1))
                    for k in range(KC):
                        wait(pe, (xT_copied, xT2_copied)[k], s)
                        for i in range(FULL + 1):
                            n = P if i < FULL else REST
                            m = nc.tensor.transpose(psum[:, 2 * k + i // 4, (i % 4) * P:(i % 4) * P + n],
                                                    x_in[0:n, u, i, k * P:(k + 1) * P], chip.ident[0:n, 0:n])
                    m.then_inc(turned, 1)

                def step(s, r, u):
                    if not (isinstance(s, int) and s == OT - 1):
                        turn(s + 1, r + u, 1 - u)
                    pe.wait_ge(xT_copied, s + 1)
                    pe.wait_ge(xT2_copied, s + 1)
                    wait(pe, oT_copied, s - 1)
                    for n in range(TAPS * KC):
                        tap, k, q = n // KC, n % KC, n % GROUPS
                        view = xT[:, u, k, :].rearrange("p (y x) -> p y x", x=S2)[:, tap // 3:tap // 3 + YT, tap % 3:tap % 3 + N]
                        m = nc.tensor.matmul(psum[q * OQ:(q + 1) * OQ, 4 + u, :], w[:, tap, k, :], view,
                                             start=(n < GROUPS), stop=(n >= TAPS * KC - GROUPS), tile_position=(0, q * OQ))
                    m.then_inc(convolved, 1)
                    pe.wait_ge(oT_copied, s + 1)
                    wait(pe, kept, s - 1)
                    for j in range(YTOK // P):
                        m = nc.tensor.matmul(psum[:, 6 + u, j * OQ:(j + 1) * OQ], oT[:, u, j * P:(j + 1) * P], stack[:],
                                             start=True, stop=True)
                    m.then_inc(added, 1)

                pe.wait_ge(weights, 16)
                turn(0, 0, 0)
                turns(pe, OT, step)

            def x_copy(copy, eng, done, k, s, u):
                eng.wait_ge(turned, s + 1)
                wait(eng, convolved, s - 1)
                copy(xT[:, u, k, :], psum[:, 2 * k:2 * k + 2, :].rearrange("p a n -> p (a n)")[:, 0:SPAN_ROWS]).then_inc(done, 1)

            @block.scalar
            def _(act):
                def copy(dst, src):
                    return nc.scalar.activation(dst, src, ACT.Copy)

                def step(s, r, u):
                    if not (isinstance(s, int) and s == OT - 1):
                        x_copy(copy, act, xT_copied, 0, s + 1, 1 - u)
                    act.wait_ge(convolved, s + 1)
                    wait(act, added, s - 1)
                    copy(oT[:, u, :], psum[:, 4 + u, :]).then_inc(oT_copied, 1)

                x_copy(copy, act, xT_copied, 0, 0, 0)
                turns(act, OT, step)

            @block.vector
            def _(dve):
                def step(s, r, u):
                    if not (isinstance(s, int) and s == OT - 1):
                        x_copy(nc.vector.tensor_copy, dve, xT2_copied, 1, s + 1, 1 - u)
                    dve.wait_ge(added, s + 1)
                    per = YTOK // P
                    nc.vector.tensor_scalar(off_all[:, bass.ds(s * per, per), :],
                                            psum[:, 6 + u, 0:per * OQ].rearrange("p (j f) -> p j f", f=OQ), 1.0, None,
                                            ALU.mult).then_inc(kept, 1)

                nc.vector.memset(w[:], 0.0).then_inc(cleared, 1)
                nc.vector.tensor_reduce(stack[:], chip.ident[:].rearrange("p (q f) -> p f q", q=GROUPS), AX.X, ALU.add)
                x_copy(nc.vector.tensor_copy, dve, xT2_copied, 1, 0, 0)
                turns(dve, OT, step)


def sample_plan(nc, chip, off_all, place, weight):
    chip.part = "plan"
    with ExitStack() as ctx:
        def sb(name, shape, dt=F32):
            return ctx.enter_context(nc.sbuf_tensor("plan_" + name, shape, dt))

        A = 2 * TAPS
        grid_i, grid = sb("grid_i", [P, TILES, A], I32), sb("grid", [P, TILES, A])
        whole_i = sb("whole_i", [P, TILES, A], I32)
        pos, base, above, held = (sb(n, [P, TILES, A]) for n in ("pos", "base", "above", "held"))
        w1, w0 = sb("w1", [P, TILES, A]), sb("w0", [P, TILES, A])
        mask = sb("mask", [P, TILES, TAPS])
        grid_ready, mask_ready = chip.sem("grid_ready"), chip.sem("mask_ready")

        with nc.Block() as block:
            @block.gpsimd
            def _(pool):
                for h in range(2):
                    half = slice(h * N, (h + 1) * N)
                    for b in range(B):
                        span = slice(b * (TILES // B), (b + 1) * (TILES // B))
                        nc.gpsimd.iota(grid_i[half, span, 0:TAPS], pattern=[[2, TILES // B], [1, 3], [0, 3]], base=h - 1,
                                       channel_multiplier=0)
                    nc.gpsimd.iota(grid_i[half, :, TAPS:A], pattern=[[0, TILES], [0, 3], [1, 3]], base=-1,
                                   channel_multiplier=1)
                nc.gpsimd.drain()
                nc.gpsimd.tensor_copy(grid[:], grid_i[:]).then_inc(grid_ready, 1)

            @block.scalar
            def _(act):
                nc.scalar.activation(mask[:], off_all[:, :, A:OFF], ACT.Sigmoid).then_inc(mask_ready, 1)

            @block.vector
            def _(dve):
                y, x = slice(0, TAPS), slice(TAPS, A)
                dve.wait_ge(grid_ready, 1)
                nc.vector.tensor_tensor(pos[:], off_all[:, :, 0:A], grid[:], ALU.add)
                dve.drain()
                nc.vector.tensor_scalar(pos[:], pos[:], -2.0, float(N + 1), ALU.max, ALU.min)
                dve.drain()
                nc.vector.tensor_copy(whole_i[:], pos[:])
                dve.drain()
                nc.vector.tensor_copy(base[:], whole_i[:])
                dve.drain()
                nc.vector.tensor_tensor(above[:], base[:], pos[:], ALU.is_gt)
                dve.drain()
                nc.vector.tensor_tensor(base[:], base[:], above[:], ALU.subtract)
                dve.drain()
                nc.vector.tensor_tensor(w1[:], pos[:], base[:], ALU.subtract)
                nc.vector.tensor_scalar(held[:], base[:], -1.0, float(N - 1), ALU.max, ALU.min)
                dve.drain()
                nc.vector.tensor_scalar(w0[:], w1[:], -1.0, 1.0, ALU.mult, ALU.add)
                nc.vector.tensor_tensor(above[:], base[:], held[:], ALU.is_equal)
                dve.drain()
                nc.vector.tensor_tensor(w1[:], w1[:], above[:], ALU.mult)
                nc.vector.tensor_tensor(w0[:], w0[:], above[:], ALU.mult)
                nc.vector.scalar_tensor_tensor(out=pos[:, :, y], in0=held[:, :, y], scalar=float(S1), in1=held[:, :, x],
                                               op0=ALU.mult, op1=ALU.add)
                dve.drain()
                dve.wait_ge(mask_ready, 1)
                for w in (w0, w1):
                    nc.vector.tensor_tensor(w[:, :, y], w[:, :, y], mask[:], ALU.mult)
                for b in range(B):
                    span = slice(b * (TILES // B), (b + 1) * (TILES // B))
                    nc.vector.tensor_scalar(place[:, span, :], pos[:, span, y], float(S1 + 1 + b * S1 * S1), None, ALU.add)
                dve.drain()
                for dy, wy in enumerate((w0, w1)):
                    for dx, wx in enumerate((w0, w1)):
                        nc.vector.tensor_tensor(weight[:, :, :, 2 * dy + dx], wy[:, :, y], wx[:, :, x], ALU.mult)
                dve.drain()


def deformable(nc, chip, corners_dram, dcn_w, gamma, beta, mean, var, place, weight, out):
    chip.part = "dcn"
    psum = chip.psum
    R = 3
    with ExitStack() as ctx:
        def sb(name, shape, dt=F32):
            return ctx.enter_context(nc.sbuf_tensor("dcn_" + name, shape, dt))

        w = sb("w", [P, TAPS, KC, C])
        pix = sb("pix", [P, 2, TAPS, 4 * C])
        at, part = sb("at", [P, 2, TAPS], I32), sb("part", [P, 2, TAPS, 4])
        blend = sb("blend", [P, R, C])
        bT = sb("bT", [P, 2, KC, P])
        mean_r, inv_r, beta_r, std_r = (sb(n, [P, C]) for n in ("mean_r", "inv_r", "beta_r", "std_r"))
        gamma_r = sb("gamma_r", [P, C])
        eps = sb("eps", [P, 1])
        y1, y2, y = sb("y1", [P, 2, C]), sb("y2", [P, 2, C]), sb("y", [P, 2, C])

        weights, eps_set, rooted, norm_ready, staged = (chip.sem(n) for n in ("weights", "eps_set", "rooted", "norm_ready", "staged"))
        passed = chip.sem("passed")
        gathered = [[chip.sem(f"gathered{u}_{t}") for t in range(TAPS)] for u in range(2)]
        first_corner, blended, turned, bT_copied, multiplied = (chip.sem(n) for n in (
            "first_corner", "blended", "turned", "bT_copied", "multiplied"))
        centred, scaled, finished = chip.sem("centred"), chip.sem("scaled"), chip.sem("finished")
        stored = [chip.sem(f"stored{u}") for u in range(2)]
        table = corners_dram.rearrange("b y x k c -> (b y x) (k c)")
        out_rows = out.rearrange("b y x c -> (b y x) c")
        last = 2 * TAPS - 1

        with nc.Block() as block:
            @block.sync
            def _(sp):
                sp.dma_start(w[:], dcn_w.rearrange("a b (k p) f -> p (a b) k f", p=P)).then_inc(weights, 16)
                for dst, v in ((mean_r, mean), (gamma_r, gamma), (beta_r, beta), (std_r, var)):
                    sp.dma_start(dst[:], across(v)).then_inc(weights, 16)
                with sp.Fori(0, TILES // 2) as r:
                    for u in range(2):
                        s = r * 2 + u
                        sp.wait_ge(finished, s + 1)
                        sp.dma_start(out_rows[bass.ds(s * P, P), :], y[:, u, :]).then_inc(stored[u], 16)
                for u in range(2):
                    sp.wait_ge(stored[u], 16 * (TILES // 2))

            @block.gpsimd
            def _(pool):
                def gather(s, r, u):
                    pool.wait_ge(staged, s + 1)
                    pool.sem_inc(passed, 1)
                    for t in range(TAPS):
                        wait(pool, blended, (s - 2) * TAPS + t + 1)
                        if not isinstance(s, int) or s >= 2:
                            pool.sem_inc(passed, 1)
                        nc.gpsimd.indirect_dma_start(pix[:, u, t, :], None, table, bass.IndirectOffsetOnAxis(
                            at[:, u, t:t + 1], 0)).then_inc(gathered[u][t], 16)

                def finish(s, r, u):
                    pool.wait_ge(centred, s + 1)
                    wait(pool, finished, s - 1)
                    nc.gpsimd.tensor_tensor(y2[:, u, :], y1[:, u, :], inv_r[:], ALU.mult).then_inc(scaled, 1)
                    pool.wait_ge(scaled, 2 * s + 1)
                    nc.gpsimd.tensor_tensor(y2[:, u, :], y2[:, u, :], beta_r[:], ALU.add).then_inc(scaled, 1)

                def step(s, r, u):
                    if not (isinstance(s, int) and s == TILES - 1):
                        gather(s + 1, r + u, 1 - u)
                    finish(s, r, u)

                gather(0, 0, 0)
                pool.wait_ge(norm_ready, 2)
                pool.wait_ge(weights, 80)
                turns(pool, TILES, step)

            @block.vector
            def _(dve):
                def stage(s, u):
                    wait(dve, first_corner, (s - 1) * TAPS)
                    nc.vector.tensor_scalar(at[:, u, :], place[:, s, :], 1.0, None, ALU.mult)
                    nc.vector.tensor_scalar(part[:, u], weight[:, s], 1.0, None, ALU.mult).then_inc(staged, 1)

                def finish(s, u):
                    dve.wait_ge(multiplied, TAPS * (s + 1))
                    wait(dve, scaled, 2 * (s - 1))
                    nc.vector.tensor_tensor(y1[:, u, :], psum[:, 4 + u, 0:C], mean_r[:], ALU.subtract).then_inc(centred, 1)

                def step(s, r, u):
                    for t in range(TAPS):
                        n, slot = s * TAPS + t, (u * TAPS + t) % R
                        if t == 2:
                            if not (isinstance(s, int) and s == 0):
                                finish(s - 1, 1 - u)
                        dve.wait_ge(gathered[u][t], 16 * (r + 1))
                        dve.wait_ge(first_corner, n + 1)
                        for k in range(1, 4):
                            m = nc.vector.scalar_tensor_tensor(
                                out=blend[:, slot, :], in0=pix[:, u, t, k * C:(k + 1) * C], scalar=part[:, u, t, k:k + 1],
                                in1=blend[:, slot, :], op0=ALU.mult, op1=ALU.add)
                            if k < 3:
                                dve.drain()
                        m.then_inc(blended, 1)
                        if t == 0 and not (isinstance(s, int) and s == TILES - 1):
                            stage(s + 1, 1 - u)

                nc.vector.memset(eps[:], 1e-3).then_inc(eps_set, 1)
                dve.wait_ge(rooted, 1)
                nc.vector.reciprocal(inv_r[:], std_r[:]).then_inc(norm_ready, 1)
                dve.wait_ge(norm_ready, 1)
                nc.vector.tensor_tensor(inv_r[:], inv_r[:], gamma_r[:], ALU.mult).then_inc(norm_ready, 1)
                stage(0, 0)
                turns(dve, TILES, step)
                finish(TILES - 1, 1)

            @block.scalar
            def _(act):
                def first(s, r, u, t):
                    n, slot = s * TAPS + t, (u * TAPS + t) % R
                    act.wait_ge(staged, s + 1)
                    act.wait_ge(gathered[u][t], 16 * (r + 1))
                    wait(act, turned, n - R + 1)
                    nc.scalar.activation(blend[:, slot, :], pix[:, u, t, 0:C], ACT.Copy,
                                         scale=part[:, u, t, 0:1]).then_inc(first_corner, 1)

                def step(s, r, u):
                    for t in range(TAPS):
                        n = s * TAPS + t
                        if t < TAPS - 1:
                            first(s, r, u, t + 1)
                        elif not (isinstance(s, int) and s == TILES - 1):
                            first(s + 1, r + u, 1 - u, 0)
                        act.wait_ge(turned, n + 1)
                        wait(act, multiplied, n - 1)
                        nc.scalar.activation(bT[:, (u * TAPS + t) % 2], psum[:, (u * TAPS + t) % 2, 0:C]
                                             .rearrange("p (k n) -> p k n", k=KC), ACT.Copy).then_inc(bT_copied, 1)
                        if t == 4 and not (isinstance(s, int) and s == 0):
                            finish(s - 1, r + u - 1, 1 - u)

                def finish(s, r, u):
                    act.wait_ge(scaled, 2 * s + 2)
                    wait(act, stored[u], 16 * r)
                    nc.scalar.activation(y[:, u, :], y2[:, u, :], ACT.Relu).then_inc(finished, 1)

                act.wait_ge(weights, 80)
                act.wait_ge(eps_set, 1)
                nc.scalar.activation(std_r[:], std_r[:], ACT.Sqrt, bias=eps[:]).then_inc(rooted, 1)
                first(0, 0, 0, 0)
                turns(act, TILES, step)
                finish(TILES - 1, TILES // 2 - 1, 1)

            @block.tensor
            def _(pe):
                def turn(s, u, t):
                    n = s * TAPS + t
                    pe.wait_ge(blended, n + 1)
                    wait(pe, bT_copied, n - 1)
                    for k in range(KC):
                        m = nc.tensor.transpose(psum[:, (u * TAPS + t) % 2, k * P:(k + 1) * P],
                                                blend[:, (u * TAPS + t) % R, k * P:(k + 1) * P], chip.ident[:])
                    m.then_inc(turned, 1)

                def step(s, r, u):
                    for t in range(TAPS):
                        if t < TAPS - 1:
                            turn(s, u, t + 1)
                        elif not (isinstance(s, int) and s == TILES - 1):
                            turn(s + 1, 1 - u, 0)
                        pe.wait_ge(bT_copied, s * TAPS + t + 1)
                        if t == 0:
                            wait(pe, centred, s - 1)
                        for k in range(KC):
                            m = nc.tensor.matmul(psum[:, 4 + u, 0:C], bT[:, (u * TAPS + t) % 2, k, :], w[:, t, k, :],
                                                 start=(t == 0 and k == 0), stop=(t == TAPS - 1 and k == KC - 1))
                        m.then_inc(multiplied, 1)

                pe.wait_ge(weights, 80)
                turn(0, 0, 0)
                turns(pe, TILES, step)


def conv_sequence(nc, x, wq, wk, wv1, wv2, wo, w1, b1, w2, b2, g_agg, be_agg, g_out, be_out,
                  kernel_f, kernel_g, kernel_h, gamma,
                  wq2, bq, wk2, bk, wv, bv, wcq, bcq, wck, bck, wcv, bcv, wp, bp,
                  offset_w, dcn_w, bn_gamma, bn_beta, mean, var, out):
    def scratch(name, shape):
        return nc.dram_tensor(name + "_dram", shape, F32, kind="Internal").ap()

    v2_dram, e_dram, r_dram = scratch("v2", [N, P, C]), scratch("e", [B, N, N, BANK]), scratch("r", [B, N, BANK])
    x1, fg, h = scratch("x1", [B, N, N, C]), scratch("fg", [2 * D, B, N, N]), scratch("h", [B, N, N, C])
    x2, qkc, v, mix_dram = scratch("x2", [B, HW, C]), scratch("qkc", [3 * D, T]), scratch("v", [T, C]), scratch("mix", [D, B, C])
    corners, padded = scratch("corners", [B, S1, S1, 4, C]), scratch("padded", [B, S2, S2, C])
    fg_parts = fg.rearrange("(a r) b y x -> a r b (y x)", a=2)
    qkc_parts = qkc.rearrange("(a r) (b n) -> a r b n", a=3, b=B)

    def load_gamma(sp, gam, mix, sem):
        sp.dma_start(gam[:], across(gamma)).then_inc(sem, 16)

    def load_mix(sp, gam, mix, sem):
        sp.dma_start(mix[:], mix_dram).then_inc(sem, 16)

    def store_x2(sp, b, t, y_slot, sem):
        sp.dma_start(x2[b, bass.ds(t * QT, QT), :].rearrange("(j p) c -> p j c", p=P), y_slot).then_inc(sem, 16)

    load_gamma.count = load_mix.count = store_x2.count = 1

    with ExitStack() as ctx:
        chip = Chip(nc, ctx)
        with nc.cleanup_on_exit():
            make_identity(nc, chip)
            clear_borders(nc, chip, corners, padded)
            triangle_scores(nc, chip, x, wq, wk, wv2, v2_dram, e_dram, r_dram)
        with nc.cleanup_on_exit():
            triangle_output(nc, chip, x, wv1, wo, w1, b1, w2, b2, g_agg, be_agg, g_out, be_out, (kernel_f, kernel_g),
                            kernel_h, v2_dram, e_dram, r_dram, x1, fg, h)
        with nc.cleanup_on_exit():
            attention(nc, chip, "attention1", fg_parts[0], fg_parts[1], h.rearrange("b y x c -> b (y x) c"),
                      x1.rearrange("b y x c -> b (y x) c"), 1.0, True, None, load_gamma, store_x2)
        with nc.cleanup_on_exit():
            project2(nc, chip, x2.rearrange("b n c -> (b n) c"), wq2, bq, wk2, bk, wv, bv, wcq, bcq, wck, bck, wcv, bcv,
                     wp, bp, qkc, v, mix_dram)
        with nc.cleanup_on_exit():
            attention(nc, chip, "attention2", qkc_parts[1], qkc_parts[0], v.rearrange("(b n) c -> b n c", b=B), x2,
                      float(CR) ** -0.5, False, qkc_parts[2], load_mix, corner_store(corners, padded))
        with nc.sbuf_tensor("off_all", [P, TILES, OQ], F32) as off_all, \
                nc.sbuf_tensor("place", [P, TILES, TAPS], F32) as place, \
                nc.sbuf_tensor("weight", [P, TILES, TAPS, 4], F32) as weight:
            with nc.cleanup_on_exit():
                offsets(nc, chip, padded, offset_w, off_all)
                sample_plan(nc, chip, off_all, place, weight)
            with nc.cleanup_on_exit():
                deformable(nc, chip, corners, dcn_w, bn_gamma, bn_beta, mean, var, place, weight, out)


_INS = ['x', 'L0_conv_Wq', 'L0_conv_Wk', 'L0_conv_Wv1', 'L0_conv_Wv2', 'L0_conv_Wo', 'L0_conv_W1', 'L0_conv_b1',
        'L0_conv_W2', 'L0_conv_b2', 'L0_conv_g_agg', 'L0_conv_be_agg', 'L0_conv_g_out', 'L0_conv_be_out',
        'L1_conv_kernel_f', 'L1_conv_kernel_g', 'L1_conv_kernel_h', 'L1_conv_gamma',
        'L2_conv_Wq', 'L2_conv_bq', 'L2_conv_Wk', 'L2_conv_bk', 'L2_conv_Wv', 'L2_conv_bv', 'L2_conv_Wcq', 'L2_conv_bcq',
        'L2_conv_Wck', 'L2_conv_bck', 'L2_conv_Wcv', 'L2_conv_bcv', 'L2_conv_Wp', 'L2_conv_bp',
        'L3_conv_offset_w', 'L3_conv_dcn_w', 'L3_conv_gamma', 'L3_conv_beta', 'L3_conv_moving_mean', 'L3_conv_moving_var']
_OUTS = [((B, N, N, C), 'float32')]


def kernel(**inputs):
    import numpy as _np
    import concourse.bacc as _bacc
    from concourse import mybir as _mybir
    from concourse.bass_utils import run_bass_kernel_spmd as _run

    nc = _bacc.Bacc("TRN2", target_bir_lowering=False, num_devices=1)
    arrays, args = {}, []
    for name in _INS:
        a = _np.ascontiguousarray(inputs[name])
        arrays[f"in_{name}_dram"] = a
        args.append(nc.dram_tensor(f"in_{name}_dram", a.shape, _mybir.dt.from_np(a.dtype), kind="ExternalInput").ap())
    for i, (shape, dtype) in enumerate(_OUTS):
        dt = _mybir.dt.from_np(_np.dtype(dtype))
        args.append(nc.dram_tensor(f"out_{i}_dram", shape, dt, kind="ExternalOutput").ap())
    conv_sequence(nc, *args)
    r = _run(nc, [arrays], core_ids=[0])
    got = tuple(r.results[0][f"out_{i}_dram"] for i in range(len(_OUTS)))
    return got[0]
```

```python
from contextlib import ExitStack

import concourse.bass as bass
from concourse import mybir

F32 = mybir.dt.float32
F32R = mybir.dt.float32r
I32 = mybir.dt.int32
U32 = mybir.dt.uint32
ACT = mybir.ActivationFunctionType
ALU = mybir.AluOpType
AX = mybir.AxisListType

P = 128
B = 2
N = 64
C = 256
KC = C // P
HW = N * N
T = B * HW
BANK = 512
HEADS = 8
DK = C // HEADS
FF = 2 * C
KF = FF // P


def wait(eng, sem, count):
    if not (isinstance(count, int) and count <= 0):
        eng.wait_ge(sem, count)


def turns(eng, count, step, unroll=2, head=1, tail=1):
    rounds = count // unroll
    for r in range(head):
        for u in range(unroll):
            step(r * unroll + u, r, u)
    with eng.Fori(head, rounds - tail) as r:
        for u in range(unroll):
            step(r * unroll + u, r, u)
    for r in range(rounds - tail, rounds):
        for u in range(unroll):
            step(r * unroll + u, r, u)


def rows(w):
    return w.rearrange("(k p) n -> p k n", p=P)


def column(v):
    return v.rearrange("(p a) -> p a", a=1)


def across(v, parts=P):
    return v.rearrange("(a n) -> a n", a=1).broadcast_to([parts, v.shape[0]])


class Chip:

    def __init__(self, nc, ctx):
        self.nc, self.ctx, self.part = nc, ctx, ""
        self.psum = ctx.enter_context(nc.psum_tensor("psum", [P, 8, BANK], F32))
        self.ident = ctx.enter_context(nc.sbuf_tensor("ident", [P, P], F32))

    def sem(self, name):
        return self.nc.alloc_semaphore(name=f"{self.part}_{name}")


def make_identity(nc, chip):
    chip.part = "start"
    zeroed, identity_ready, cleared = (chip.sem(n) for n in ("zeroed", "identity_ready", "psum_cleared"))
    with nc.Block() as block:
        @block.gpsimd
        def _(pool):
            nc.gpsimd.memset(chip.ident[:], 0.0).then_inc(zeroed, 1)
            pool.wait_ge(zeroed, 1)
            nc.gpsimd.affine_select(out=chip.ident[:], in_=chip.ident[:], compare_op=ALU.not_equal, fill=1.0,
                                    base=0, pattern=[[-1, P]], channel_multiplier=1).then_inc(identity_ready, 1)
            pool.wait_ge(identity_ready, 1)

        @block.vector
        def _(dve):
            nc.vector.memset(chip.psum[:], 0.0).then_inc(cleared, 1)
            dve.wait_ge(cleared, 1)


def triangle_scores(nc, chip, x, wq, wk, wv2, v2_dram, e_dram, r_dram):
    chip.part = "scores"
    psum = chip.psum
    with ExitStack() as ctx:
        def sb(name, shape, dt=F32):
            return ctx.enter_context(nc.sbuf_tensor(name, shape, dt))

        wq_sb, wk_sb, wv_sb = sb("wq_sb", [P, KC, C]), sb("wk_sb", [P, KC, C]), sb("wv2_sb", [P, KC, C])
        x_in = sb("x_in", [P, 2, 2, C])
        xT = sb("xT", [P, 2, KC, P])
        qk = sb("qk", [P, 4, P])
        v_out = sb("v_out", [P, 2, C])
        S = sb("S", [P, N, BANK])
        top = sb("top", [P, BANK])
        part_sum = sb("part_sum", [P, 4, BANK])
        denom = sb("denom", [P, BANK])
        inverse = sb("inverse", [P, BANK])

        weights = chip.sem("weights")
        loaded = [chip.sem(f"loaded{u}") for u in range(2)]
        stored = [chip.sem(f"stored{u}") for u in range(2)]
        transposed, xT_copied = chip.sem("transposed"), chip.sem("xT_copied")
        qk_done, qk_copied = chip.sem("qk_done"), chip.sem("qk_copied")
        v_done, v_copied = chip.sem("v_done"), chip.sem("v_copied")
        scores_done, scores_copied, maxed = chip.sem("scores_done"), chip.sem("scores_copied"), chip.sem("maxed")

        with nc.Block() as block:
            @block.sync
            def _(sp):
                for w, dst in ((wq, wq_sb), (wk, wk_sb), (wv2, wv_sb)):
                    sp.dma_start(dst[:], rows(w)).then_inc(weights, 16)

                def load(s, u):
                    for b in range(B):
                        half = slice(b * N, (b + 1) * N)
                        sp.dma_start(x_in[half, u, 0, :], x[b, s]).then_inc(loaded[u], 16)
                        sp.dma_start(x_in[half, u, 1, :], x[b, :, s]).then_inc(loaded[u], 16)

                def step(s, r, u, more=True):
                    if more:
                        sp.wait_ge(transposed, s + 1)
                        load(s + 2, u)
                    sp.wait_ge(v_copied, s + 1)
                    sp.dma_start(v2_dram[s], v_out[:, u, :]).then_inc(stored[u], 16)

                load(0, 0)
                load(1, 1)
                with sp.Fori(0, N // 2 - 1) as r:
                    for u in range(2):
                        step(r * 2 + u, r, u)
                for u in range(2):
                    step(N - 2 + u, N // 2 - 1, u, more=False)
                for u in range(2):
                    sp.wait_ge(stored[u], 16 * (N // 2))

            @block.tensor
            def _(pe):
                def transposes(s, r, u):
                    pe.wait_ge(loaded[u], 64 * (r + 1))
                    wait(pe, xT_copied, s)
                    for side in range(2):
                        for k in range(KC):
                            m = nc.tensor.transpose(psum[:, 0, (2 * side + k) * P:(2 * side + k + 1) * P],
                                                    x_in[:, u, side, k * P:(k + 1) * P], chip.ident[:])
                    m.then_inc(transposed, 1)

                def step(s, r, u):
                    pe.wait_ge(xT_copied, s + 1)
                    wait(pe, qk_copied, s)
                    for side, w, at in ((1, wq_sb, 0), (0, wk_sb, 2)):
                        for t in range(2):
                            for k in range(KC):
                                m = nc.tensor.matmul(psum[:, 1, (at + t) * P:(at + t + 1) * P],
                                                     w[:, k, t * P:(t + 1) * P], xT[:, side, k, :],
                                                     start=(k == 0), stop=(k == KC - 1))
                    m.then_inc(qk_done, 1)
                    wait(pe, v_copied, s)
                    for k in range(KC):
                        m = nc.tensor.matmul(psum[:, 2, 0:C], xT[:, 1, k, :], wv_sb[:, k, :],
                                             start=(k == 0), stop=(k == KC - 1))
                    m.then_inc(v_done, 1)
                    if not (isinstance(s, int) and s == N - 1):
                        transposes(s + 1, r + u, 1 - u)
                    pe.wait_ge(qk_copied, s + 1)
                    wait(pe, scores_copied, s)
                    for t in range(2):
                        for g in range(4):
                            for b in range(B):
                                head, toks = slice(32 * g, 32 * g + 32), slice(b * N, (b + 1) * N)
                                m = nc.tensor.matmul(psum[toks, 3 + g, t * N:(t + 1) * N],
                                                     qk[head, t, toks], qk[head, 2 + t, toks],
                                                     start=True, stop=True)
                    m.then_inc(scores_done, 1)

                pe.wait_ge(weights, 48)
                transposes(0, 0, 0)
                turns(pe, N, step)

            @block.scalar
            def _(act):
                def x_copy(s):
                    act.wait_ge(transposed, s + 1)
                    wait(act, v_done, s)
                    nc.scalar.activation(xT[:].rearrange("p a k n -> p (a k n)"), psum[:, 0, :],
                                         ACT.Copy).then_inc(xT_copied, 1)

                def step(s, r, u):
                    act.wait_ge(v_done, s + 1)
                    wait(act, stored[u], r * 16)
                    nc.scalar.activation(v_out[:, u, :], psum[:, 2, 0:C], ACT.Copy).then_inc(v_copied, 1)
                    if not (isinstance(s, int) and s == N - 1):
                        x_copy(s + 1)
                    act.wait_ge(scores_done, s + 1)
                    nc.scalar.activation(S[:, s, :].rearrange("p (g n) -> p g n", g=4), psum[:, 3:7, 0:P],
                                         ACT.Copy).then_inc(scores_copied, 1)

                x_copy(0)
                turns(act, N, step)

            @block.vector
            def _(dve):
                def step(s, r, u):
                    dve.wait_ge(qk_done, s + 1)
                    wait(dve, scores_done, s)
                    nc.vector.tensor_copy(qk[:].rearrange("p a n -> p (a n)"), psum[:, 1, :]).then_inc(qk_copied, 1)
                    dve.wait_ge(scores_copied, s + 1)
                    if isinstance(s, int) and s == 0:
                        nc.vector.tensor_copy(top[:], S[:, 0, :]).then_inc(maxed, 1)
                    else:
                        dve.wait_ge(maxed, s)
                        nc.vector.tensor_tensor(top[:], top[:], S[:, s, :], ALU.max).then_inc(maxed, 1)

                turns(dve, N, step)

        chip.part = "softmax0"
        (shifted, shifted2, raised, summed, psum_summed, e_stored) = (chip.sem(n) for n in (
            "shifted", "shifted2", "raised", "summed", "psum_summed", "e_stored"))
        CH = 8
        JN = N // CH
        POOL_SHIFTS = (5, 7)
        DVE_SUMS = (2, 4, 6)

        def piece(c):
            return S[:, c * JN:(c + 1) * JN, :]

        with nc.Block() as block:
            def shift(engine, c, done):
                engine.tensor_tensor(piece(c), piece(c), top[:, None, :].broadcast_to([P, JN, BANK]),
                                     ALU.subtract).then_inc(done, 1)

            @block.gpsimd
            def _(pool):
                for c in POOL_SHIFTS:
                    shift(nc.gpsimd, c, shifted2)

            @block.vector
            def _(dve):
                def sums(c):
                    dve.wait_ge(raised, c + 1)
                    nc.vector.tensor_reduce(part_sum[:, DVE_SUMS.index(c), :], piece(c).rearrange("p j n -> p n j"),
                                            AX.X, ALU.add).then_inc(summed, 1)

                for c in range(CH):
                    if c not in POOL_SHIFTS:
                        shift(nc.vector, c, shifted)
                    if c - 2 in DVE_SUMS:
                        sums(c - 2)
                sums(DVE_SUMS[-1])
                dve.wait_ge(psum_summed, 1)
                nc.vector.tensor_copy(part_sum[:, 3, :], psum[:, 7, :]).then_inc(summed, 1)
                dve.wait_ge(summed, 4)
                nc.vector.tensor_reduce(denom[:], part_sum[:].rearrange("p c n -> p n c"), AX.X,
                                        ALU.add).then_inc(summed, 1)
                dve.wait_ge(summed, 5)
                nc.vector.reciprocal(inverse[:], denom[:]).then_inc(summed, 1)

            @block.scalar
            def _(act):
                for c in range(CH):
                    if c in POOL_SHIFTS:
                        act.wait_ge(shifted2, POOL_SHIFTS.index(c) + 1)
                    else:
                        act.wait_ge(shifted, c + 1 - sum(d < c for d in POOL_SHIFTS))
                    at = piece(c).rearrange("p j n -> p (j n)")
                    nc.scalar.activation(at, at, ACT.Exp, scale=float(DK) ** -0.5).then_inc(raised, 1)

            @block.tensor
            def _(pe):
                mine = [c for c in range(CH) if c not in DVE_SUMS]
                for c in mine:
                    pe.wait_ge(raised, c + 1)
                    for j in range(c * JN, (c + 1) * JN):
                        m = nc.tensor.matmul(psum[:, 7, :], chip.ident[:], S[:, j, :], start=(j == mine[0] * JN),
                                             stop=(j == (mine[-1] + 1) * JN - 1))
                m.then_inc(psum_summed, 1)

            @block.sync
            def _(sp):
                for c in range(CH):
                    sp.wait_ge(raised, c + 1)
                    for b in range(B):
                        sp.dma_start(e_dram[b, :, c * JN:(c + 1) * JN, :],
                                     S[b * N:(b + 1) * N, c * JN:(c + 1) * JN, :]).then_inc(e_stored, 16)
                sp.wait_ge(summed, 6)
                sp.dma_start(r_dram.rearrange("b i n -> (b i) n"), inverse[:]).then_inc(e_stored, 16)
                sp.wait_ge(e_stored, 16 * (CH * B + 1))


def active(turn, first, last):
    return not isinstance(turn, int) or first <= turn <= last


def triangle_output(nc, chip, x, wv1, wo, w1, b1, w2, b2, g_agg, be_agg, g_out, be_out, w_fg, w_h,
                    v2_dram, e_dram, r_dram, x1_dram, fg_dram, h_dram):
    chip.part = "out0"
    psum = chip.psum
    LC = 8
    NCH = N // LC
    WS = 5
    FG = w_fg[0].shape[1] + w_fg[1].shape[1]
    with ExitStack() as ctx:
        def sb(name, shape, dt=F32):
            return ctx.enter_context(nc.sbuf_tensor(name, shape, dt))

        wv_sb, wo_sb, wh_sb = sb("wv1_sb", [P, KC, C]), sb("wo_sb", [P, KC, C]), sb("wh_sb", [P, KC, C])
        w1_sb, w2_sb, wfg_sb = sb("w1_sb", [P, KC, FF]), sb("w2_sb", [P, KF, C]), sb("wfg_sb", [P, KC, FG])
        b1_sb, eps = sb("b1_sb", [P, KF]), sb("eps", [P, 1])
        norms = {n: sb(n, [P, C]) for n in ("gain1", "shift1", "bias2", "gain2", "shift2")}
        V2 = sb("V2", [P, N, C])
        W = sb("W", [P, WS, LC, C])
        W_last = sb("W_last", [P, LC, C])
        x_in, x_res, xT, v1 = sb("x_row", [P, 2, C]), sb("x_res", [P, 2, C]), sb("x_rowT", [P, KC, P]), sb("v1", [P, 2, C])
        e_in = sb("e_in", [P, 2, BANK])
        r_in = sb("r_in", [P, 2, B, BANK])
        att = sb("att", [P, 2, B, BANK])
        o = sb("o", [P, 2, BANK])
        OT = sb("OT", [P, 2, 2, B, N])
        res1, res2 = sb("res1", [P, C]), sb("res2", [P, C])
        stat1, stat2 = sb("stat1", [P, 6]), sb("stat2", [P, 6])
        mv1, mv2 = sb("mv1", [P, 2]), sb("mv2", [P, 2])
        sd1, sd2, rs1, rs2 = (sb(n, [P, 1]) for n in ("sd1", "sd2", "rs1", "rs2"))
        hn, hg, h1, h1b = (sb(n, [P, C]) for n in ("hn", "hg", "h1", "h1b"))
        xn, xg, x1 = sb("xn", [P, C]), sb("xg", [P, C]), sb("x1", [P, 2, C])
        h1T, uT, x1T = sb("h1T", [P, KC, P]), sb("uT", [P, KF, P]), sb("x1T", [P, KC, P])
        fg_out, h_out = sb("fg_out", [FG, 2, P]), sb("h_out", [P, 2, C])

        wv_loaded, weights, v2_loaded = chip.sem("wv_loaded"), chip.sem("weights"), [chip.sem(f"v2_loaded{c}") for c in range(NCH)]
        loaded = [chip.sem(f"loaded{u}") for u in range(2)]
        res_loaded = [chip.sem(f"res_loaded{u}") for u in range(2)]
        x1_stored = [chip.sem(f"x1_stored{u}") for u in range(2)]
        fgh_stored = [chip.sem(f"fgh_stored{u}") for u in range(2)]
        (cleared, transposed, xT_copied, v1_done, v1_copied, att_ready, w_done, w_last_done, pv_done, o_copied, o_transposed,
         o_spread, attn_done, attn_read, stats1, root1, norm1, h1_steps, h1_transposed, h1T_copied,
         up_done, relu_done, ffn_done, ffn_read, stats2, root2, norm2, x1_steps, x1_transposed, x1T_copied,
         fgh_done, fgh_copied) = (chip.sem(n) for n in (
             "cleared transposed xT_copied v1_done v1_copied att_ready w_done w_last_done pv_done o_copied o_transposed "
             "o_spread attn_done attn_read stats1 root1 norm1 h1_steps h1_transposed h1T_copied "
             "up_done relu_done ffn_done ffn_read stats2 root2 norm2 x1_steps x1_transposed x1T_copied "
             "fgh_done fgh_copied").split())

        def all_turns(eng, step):
            turns(eng, N + 4, step, head=3, tail=3)

        def slot(r, u, by):
            return (u + by) % 2, r + (u + by) // 2

        def slot_back(c):
            return WS if c >= WS else NCH - max(d for d in range(NCH - 1) if d % WS == c) + c

        with nc.Block() as block:
            @block.sync
            def _(sp):
                def load(i, u):
                    for b in range(B):
                        half = slice(b * N, (b + 1) * N)
                        sp.dma_start(x_in[half, u, :], x[b, i]).then_inc(loaded[u], 16)
                        sp.dma_start(e_in[half, u, :], e_dram[b, i]).then_inc(loaded[u], 16)
                        sp.dma_start(r_in[half, u, b, :], r_dram[b, i][None, :].broadcast_to([N, BANK])).then_inc(loaded[u], 16)

                def step(i, r, u):
                    v, _ = slot(r, u, -3)
                    if active(i, 0, N - 3):
                        wait(sp, transposed, i + 1)
                        wait(sp, att_ready, i + 1)
                        load(i + 2, u)
                    if active(i, 0, N - 1):
                        wait(sp, attn_read, i - 1)
                        for b in range(B):
                            sp.dma_start(x_res[b * N:(b + 1) * N, u, :], x[b, i]).then_inc(res_loaded[u], 16)
                    if active(i, 3, N + 2):
                        m = i - 3
                        sp.wait_ge(x1_steps, 2 * m + 2)
                        for b in range(B):
                            sp.dma_start(x1_dram[b, m], x1[b * N:(b + 1) * N, v, :]).then_inc(x1_stored[v], 16)
                        sp.wait_ge(fgh_copied, 2 * m + 2)
                        for b in range(B):
                            half = slice(b * N, (b + 1) * N)
                            sp.dma_start(fg_dram[:, b, m, :], fg_out[:, v, half]).then_inc(fgh_stored[v], 16)
                            sp.dma_start(h_dram[b, m], h_out[half, v, :]).then_inc(fgh_stored[v], 16)

                sp.wait_ge(cleared, 2)
                sp.dma_start(wv_sb[:], rows(wv1)).then_inc(wv_loaded, 16)
                load(0, 0)
                load(1, 1)
                for w, dst in ((wo, wo_sb), (w1, w1_sb), (w2, w2_sb), (w_h, wh_sb)):
                    sp.dma_start(dst[:], rows(w)).then_inc(weights, 16)
                at = 0
                for w in w_fg:
                    sp.dma_start(wfg_sb[:, :, at:at + w.shape[1]], rows(w)).then_inc(weights, 16)
                    at += w.shape[1]
                with nc.allow_non_contiguous_dma(reason="a bias of 512 words, once"):
                    sp.dma_start(b1_sb[:], b1.rearrange("(k p) -> p k", p=P)).then_inc(weights, 16)
                for name, v in (("gain1", g_agg), ("shift1", be_agg), ("bias2", b2), ("gain2", g_out), ("shift2", be_out)):
                    sp.dma_start(norms[name][:], across(v)).then_inc(weights, 16)
                all_turns(sp, step)
                for u in range(2):
                    sp.wait_ge(x1_stored[u], 16 * B * (N // 2))
                    sp.wait_ge(fgh_stored[u], 32 * B * (N // 2))

            @block.tensor
            def _(pe):
                def turn_over(src, done):
                    for k in range(KC):
                        m_ = nc.tensor.transpose(psum[:, 0, k * P:(k + 1) * P], src[:, k * P:(k + 1) * P], chip.ident[:])
                    m_.then_inc(done, 1)

                def products(i, u, c):
                    n = i * NCH + c
                    if c == 0:
                        pe.wait_ge(att_ready, i + 1)
                    if c < NCH - 1:
                        pe.wait_ge(w_done, i * (NCH - 1) + c + 1)
                    else:
                        pe.wait_ge(w_last_done, i + 1)
                    wait(pe, o_copied, n - 1)
                    for l in range(LC):
                        q, g = l % 4, l // 4
                        m_ = nc.tensor.matmul(psum[32 * q:32 * q + B * HEADS, 3 + c % 2, g * C:(g + 1) * C],
                                              att[:, u, :, :].rearrange("p b (h l) -> p (b h) l", l=N)[:, :, c * LC + l],
                                              (W[:, c % WS] if c < NCH - 1 else W_last)[:, l, :], start=True, stop=True)
                    m_.then_inc(pv_done, 1)

                def turn_around(n, c):
                    pe.wait_ge(o_copied, n + 1)
                    wait(pe, o_spread, n - 1)
                    for g in range(2):
                        for t in range(2):
                            m_ = nc.tensor.transpose(psum[:, 5 + c % 2, (2 * t + g) * P:(2 * t + g + 1) * P],
                                                     o[:, c % 2, (2 * g + t) * P:(2 * g + t + 1) * P], chip.ident[:])
                    m_.then_inc(o_transposed, 1)

                def step(i, r, u):
                    if isinstance(i, int) and i == 1:
                        pe.wait_ge(weights, 16 * 12)
                    for c in range(NCH):
                        if active(i, 0, N - 1):
                            products(i, u, c)
                        if (c > 0 and active(i, 0, N - 1)) or (c == 0 and active(i, 1, N)):
                            turn_around(i * NCH + c - 1, (c - 1) % NCH)
                        if c == 0 and active(i, 0, N - 2):
                            v, vr = slot(r, u, 1)
                            pe.wait_ge(loaded[v], 16 * 6 * (vr + 1))
                            wait(pe, fgh_copied, 2 * (i - 3))
                            turn_over(x_in[:, v], transposed)
                        if c == 1 and active(i, 0, N - 2):
                            pe.wait_ge(xT_copied, i + 2)
                            wait(pe, relu_done, i - 2)
                            for k in range(KC):
                                m_ = nc.tensor.matmul(psum[:, 1, 0:C], xT[:, k, :], wv_sb[:, k, :],
                                                      start=(k == 0), stop=(k == KC - 1))
                            m_.then_inc(v1_done, 1)
                        if c == 1 and active(i, 1, N):
                            m, (v, _) = i - 1, slot(r, u, -1)
                            pe.wait_ge(o_spread, i * NCH)
                            wait(pe, attn_read, m)
                            for k in range(KC):
                                m_ = nc.tensor.matmul(psum[:, 2, 0:C], OT[:, v, k].rearrange("p b l -> p (b l)"),
                                                      wo_sb[:, k, :], start=(k == 0), stop=(k == KC - 1))
                            m_.then_inc(attn_done, 1)
                        if c == 2 and active(i, 2, N + 1):
                            m = i - 2
                            pe.wait_ge(h1_steps, 3 * m + 2)
                            if active(i, 0, N - 2):
                                pe.wait_ge(xT_copied, i + 2)
                            wait(pe, fgh_copied, 2 * (m - 1))
                            turn_over(h1, h1_transposed)
                        if c == 3 and active(i, 2, N + 1):
                            m = i - 2
                            pe.wait_ge(h1T_copied, m + 1)
                            if active(i, 0, N - 2):
                                pe.wait_ge(v1_copied, i + 2)
                            for f in range(KF):
                                for k in range(KC):
                                    m_ = nc.tensor.matmul(psum[:, 1, f * P:(f + 1) * P], w1_sb[:, k, f * P:(f + 1) * P],
                                                          h1T[:, k, :], start=(k == 0), stop=(k == KC - 1))
                            m_.then_inc(up_done, 1)
                        if c == 4 and active(i, 2, N + 1):
                            m = i - 2
                            pe.wait_ge(relu_done, m + 1)
                            wait(pe, ffn_read, m)
                            for f in range(KF):
                                m_ = nc.tensor.matmul(psum[:, 7, 0:C], uT[:, f, :], w2_sb[:, f, :],
                                                      start=(f == 0), stop=(f == KF - 1))
                            m_.then_inc(ffn_done, 1)
                        if c == 6 and active(i, 3, N + 2):
                            m, (v, _) = i - 3, slot(r, u, -3)
                            pe.wait_ge(x1_steps, 2 * m + 2)
                            if active(i, 2, N + 1):
                                pe.wait_ge(h1T_copied, i - 1)
                            turn_over(x1[:, v], x1_transposed)
                        if c == 7 and active(i, 3, N + 2):
                            pe.wait_ge(x1T_copied, i - 2)
                            for k in range(KC):
                                nc.tensor.matmul(psum[0:FG, 0, 0:P], wfg_sb[:, k, :], x1T[:, k, :],
                                                 start=(k == 0), stop=(k == KC - 1))
                            for k in range(KC):
                                m_ = nc.tensor.matmul(psum[:, 0, P:P + C], x1T[:, k, :], wh_sb[:, k, :],
                                                      start=(k == 0), stop=(k == KC - 1))
                            m_.then_inc(fgh_done, 1)

                pe.wait_ge(wv_loaded, 16)
                pe.wait_ge(loaded[0], 16 * 6)
                turn_over(x_in[:, 0], transposed)
                pe.wait_ge(xT_copied, 1)
                for k in range(KC):
                    m_ = nc.tensor.matmul(psum[:, 1, 0:C], xT[:, k, :], wv_sb[:, k, :], start=(k == 0), stop=(k == KC - 1))
                m_.then_inc(v1_done, 1)
                all_turns(pe, step)

            @block.scalar
            def _(act):
                def turned(dst, done):
                    nc.scalar.activation(dst[:], psum[:, 0, 0:C].rearrange("p (k n) -> p k n", k=KC), ACT.Copy).then_inc(done, 1)

                def x_copy(i):
                    act.wait_ge(transposed, i + 1)
                    wait(act, v1_done, i)
                    turned(xT, xT_copied)

                def v1_copy(i, u):
                    act.wait_ge(v1_done, i + 1)
                    wait(act, w_done, (i - 1) * (NCH - 1))
                    wait(act, w_last_done, i - 1)
                    nc.scalar.activation(v1[:, u, :], psum[:, 1, 0:C], ACT.Copy).then_inc(v1_copied, 1)

                def spread(n, c, i, u):
                    act.wait_ge(o_transposed, n + 1)
                    if c == 0:
                        wait(act, attn_done, i - 1)
                    for g in range(4):
                        rows_ = slice(32 * g, 32 * g + 32)
                        base = psum[rows_, 5 + c % 2, 2 * g:2 * g + 1]
                        own = bass.AP(base.tensor, base.offset, [base.ap[0], [257, 2], [8, B], [32, LC]])
                        m_ = nc.scalar.activation(OT[rows_, u, :, :, c * LC:(c + 1) * LC], own, ACT.Copy)
                    m_.then_inc(o_spread, 1)

                def root(var, sd, ready, count, done):
                    act.wait_ge(ready, count)
                    nc.scalar.activation(sd[:], var, ACT.Sqrt, bias=eps[:]).then_inc(done, 1)

                def step(i, r, u):
                    if isinstance(i, int) and i == 1:
                        act.wait_ge(weights, 16 * 12)
                    for c in range(NCH):
                        n = i * NCH + c
                        if active(i, 0, N - 1):
                            act.wait_ge(pv_done, n + 1)
                            wait(act, o_transposed, n - 1)
                            nc.scalar.activation(o[:, c % 2, :], psum[:, 3 + c % 2, :], ACT.Copy).then_inc(o_copied, 1)
                        if c > 0 and active(i, 0, N - 1):
                            spread(n - 1, c - 1, i, u)
                        if c == 0 and active(i, 1, N):
                            spread(n - 1, NCH - 1, i - 1, slot(r, u, -1)[0])
                        if c == 1 and active(i, 3, N + 2):
                            root(mv2[:, 1:2], sd2, stats2, 3 * (i - 3) + 2, root2)
                        if c == 2 and active(i, 2, N + 1):
                            m = i - 2
                            act.wait_ge(h1_transposed, m + 1)
                            wait(act, up_done, m)
                            turned(h1T, h1T_copied)
                        if c == 3 and active(i, 2, N + 1):
                            m = i - 2
                            act.wait_ge(up_done, m + 1)
                            wait(act, ffn_done, m)
                            for f in range(KF):
                                m_ = nc.scalar.activation(uT[:, f, :], psum[:, 1, f * P:(f + 1) * P], ACT.Relu,
                                                          bias=b1_sb[:, f:f + 1])
                            m_.then_inc(relu_done, 1)
                        if c == 0 and active(i, 0, N - 2):
                            x_copy(i + 1)
                        if c == 1 and active(i, 0, N - 2):
                            v1_copy(i + 1, 1 - u)
                        if c == 5 and active(i, 1, N):
                            root(mv1[:, 1:2], sd1, stats1, 3 * (i - 1) + 2, root1)
                        if c == 6 and active(i, 3, N + 2):
                            m = i - 3
                            act.wait_ge(x1_transposed, m + 1)
                            wait(act, fgh_done, m)
                            turned(x1T, x1T_copied)
                        if c == 7 and active(i, 3, N + 2):
                            m, (v, vr) = i - 3, slot(r, u, -3)
                            act.wait_ge(fgh_done, m + 1)
                            wait(act, fgh_stored[v], 32 * B * vr)
                            nc.scalar.activation(fg_out[:, v, :], psum[0:FG, 0, 0:P], ACT.Copy).then_inc(fgh_copied, 1)
                            nc.scalar.activation(h_out[:, v, :], psum[:, 0, P:P + C], ACT.Copy).then_inc(fgh_copied, 1)

                act.wait_ge(cleared, 2)
                x_copy(0)
                v1_copy(0, 0)
                all_turns(act, step)

            @block.vector
            def _(dve):
                def normalise(rs, sd, steps, m, out, res, mv, done):
                    nc.vector.reciprocal(rs[:], sd[:]).then_inc(steps, 1)
                    dve.wait_ge(steps, 3 * m + 3)
                    nc.vector.tensor_scalar(out[:], res[:], mv[:, 0:1], rs[:], ALU.subtract, ALU.mult).then_inc(done, 1)

                def statistics(res, stat, mv, read, m, steps):
                    dve.wait_ge(read, m + 1)
                    nc.vector.bn_stats(stat[:], res[:]).then_inc(steps, 1)
                    dve.drain()
                    nc.vector.bn_aggr(mv[:], stat[:]).then_inc(steps, 1)

                def step(i, r, u):
                    for c in range(NCH):
                        n = i * NCH + c
                        if c < NCH - 1 and active(i, 0, N - 1):
                            if c == 0:
                                dve.wait_ge(v1_copied, i + 1)
                            if isinstance(i, int) and i == 0:
                                dve.wait_ge(v2_loaded[c], 16)
                            wait(dve, pv_done, n - slot_back(c) + 1)
                            nc.vector.tensor_tensor(W[:, c % WS], V2[:, c * LC:(c + 1) * LC, :],
                                                    v1[:, u, None, :].broadcast_to([P, LC, C]),
                                                    ALU.mult).then_inc(w_done, 1)
                        if c == 0 and active(i, 3, N + 2):
                            m = i - 3
                            dve.wait_ge(ffn_done, m + 1)
                            dve.wait_ge(h1_steps, 3 * m + 3)
                            wait(dve, norm2, m)
                            nc.vector.tensor_tensor(res2[:], psum[:, 7, 0:C], h1b[:], ALU.add).then_inc(ffn_read, 1)
                            statistics(res2, stat2, mv2, ffn_read, m, stats2)
                        if c == 1 and active(i, 2, N + 1):
                            m = i - 2
                            dve.wait_ge(root1, m + 1)
                            wait(dve, h1_steps, 3 * m)
                            normalise(rs1, sd1, stats1, m, hn, res1, mv1, norm1)
                        if c == 4 and active(i, 3, N + 2):
                            m = i - 3
                            dve.wait_ge(root2, m + 1)
                            wait(dve, x1_steps, 2 * m)
                            normalise(rs2, sd2, stats2, m, xn, res2, mv2, norm2)
                        if c == 5 and active(i, 1, N):
                            m, (v, vr) = i - 1, slot(r, u, -1)
                            dve.wait_ge(attn_done, m + 1)
                            dve.wait_ge(res_loaded[v], 16 * B * (vr + 1))
                            wait(dve, norm1, m)
                            nc.vector.tensor_tensor(res1[:], psum[:, 2, 0:C], x_res[:, v, :],
                                                    ALU.add).then_inc(attn_read, 1)
                            statistics(res1, stat1, mv1, attn_read, m, stats1)

                nc.vector.memset(eps[:], 1e-5).then_inc(cleared, 1)
                nc.vector.memset(r_in[:], 0.0).then_inc(cleared, 1)
                all_turns(dve, step)

            @block.gpsimd
            def _(pool):
                def attention(i, r, u):
                    pool.wait_ge(loaded[u], 16 * 6 * (r + 1))
                    wait(pool, pv_done, (i - 1) * NCH)
                    nc.gpsimd.tensor_tensor(att[:, u], e_in[:, u, None, :].broadcast_to([P, B, BANK]), r_in[:, u],
                                            ALU.mult).then_inc(att_ready, 1)

                def step(i, r, u):
                    if isinstance(i, int) and i == 1:
                        pool.wait_ge(weights, 16 * 12)
                    if active(i, 2, N + 1):
                        m = i - 2
                        pool.wait_ge(norm1, m + 1)
                        wait(pool, h1_steps, 3 * m)
                        nc.gpsimd.tensor_tensor(hg[:], hn[:], norms["gain1"][:], ALU.mult).then_inc(h1_steps, 1)
                        pool.wait_ge(h1_steps, 3 * m + 1)
                        wait(pool, h1_transposed, m)
                        nc.gpsimd.tensor_tensor(h1[:], hg[:], norms["shift1"][:], ALU.add).then_inc(h1_steps, 1)
                        pool.wait_ge(h1_steps, 3 * m + 2)
                        wait(pool, ffn_read, m)
                        nc.gpsimd.tensor_tensor(h1b[:], h1[:], norms["bias2"][:], ALU.add).then_inc(h1_steps, 1)
                    if active(i, 0, N - 1):
                        pool.wait_ge(v1_copied, i + 1)
                        wait(pool, pv_done, i * NCH)
                        nc.gpsimd.tensor_tensor(W_last[:], V2[:, (NCH - 1) * LC:NCH * LC, :],
                                                v1[:, u, None, :].broadcast_to([P, LC, C]), ALU.mult).then_inc(w_last_done, 1)
                    if active(i, 3, N + 2):
                        m, (v, vr) = i - 3, slot(r, u, -3)
                        pool.wait_ge(norm2, m + 1)
                        nc.gpsimd.tensor_tensor(xg[:], xn[:], norms["gain2"][:], ALU.mult).then_inc(x1_steps, 1)
                        pool.wait_ge(x1_steps, 2 * m + 1)
                        wait(pool, x1_transposed, m - 1)
                        wait(pool, x1_stored[v], 16 * B * vr)
                        nc.gpsimd.tensor_tensor(x1[:, v, :], xg[:], norms["shift2"][:], ALU.add).then_inc(x1_steps, 1)
                    if active(i, 0, N - 2):
                        nu, nr = slot(r, u, 1)
                        attention(i + 1, nr, nu)

                for c in range(NCH):
                    if c == 2:
                        attention(0, 0, 0)
                        pool.wait_ge(wv_loaded, 16)
                    ls = slice(c * LC, (c + 1) * LC)
                    pool.dma_start(V2[:, ls, :], v2_dram[ls].rearrange("l p c -> p l c")).then_inc(v2_loaded[c], 16)
                pool.wait_ge(v2_loaded[NCH - 1], 16)
                all_turns(pool, step)


QT = 512
NT = HW // QT
SUB = QT // P
MT = HW // P
MC = HW // BANK
D = 32
RING = 4


def attention(nc, chip, name, k_dram, q_dram, v_dram, x_dram, scale, gamma, channel, load_first, store):
    chip.part = name
    psum = chip.psum
    MAXU = SUB * MC
    units = ["max"] * MAXU + (["channel"] * SUB if channel else []) + ["turn"] * 2
    NU = len(units)
    Q_AT = 5
    SPAN = 16
    unit_at = [[] for _ in range(MT)]
    for n in range(MAXU):
        unit_at[Q_AT + 2 + n * SPAN // MAXU].append(n)
    for n in range(MAXU, NU - 2):
        unit_at[Q_AT + 2 + SPAN + n - MAXU].append(n)
    for n in (NU - 2, NU - 1):
        unit_at[MT - 4].append(n)
    VP = 2
    NP = MT // VP
    VL = 4
    K_PIECE = 512
    SWITCH = NT - 1
    LAST = B * NT - 1
    SET_UP = 4
    K_READY = (1, 1 + HW // K_PIECE)
    assert B == 2
    with ExitStack() as ctx:
        def sb(tag, shape, dt=F32):
            return ctx.enter_context(nc.sbuf_tensor(f"{name}_{tag}", shape, dt))

        k_raw, v_raw = sb("k_raw", [D, HW]), sb("v_raw", [P, 2, VL * VP, C])
        K = sb("K", [3 * D + 2, B, HW], F32R)
        Q = sb("Q", [3 * D + 2, 2, QT], F32R)
        V_hi, V_lo = sb("V_hi", [P, MT, C + 2], F32R), sb("V_lo", [P, MT, C], F32R)
        q_raw, x_in = sb("q_raw", [D, 2, QT]), sb("x_in", [P, 2, SUB, C])
        e, e_hi, e_lo = sb("e", [P, RING, QT]), sb("e_hi", [P, RING, QT], F32R), sb("e_lo", [P, RING, QT], F32R)
        tops, top, minus = sb("tops", [P, SUB, MC]), sb("top", [P, SUB]), sb("minus", [P, SUB, 1])
        minus2 = sb("minus2", [P, SUB, 2], F32R)
        inv, inv_g, gam = sb("inv", [P, SUB]), sb("inv_g", [P, SUB]), sb("gam", [P, 1])
        y = sb("y", [P, 2, SUB, C])
        if channel:
            cvT, mix = sb("cvT", [D, 2, QT]), sb("mix", [D, B, C])
            CV, MIX = sb("CV", [3 * D, 2, QT], F32R), sb("MIX", [3 * D, B, C], F32R)

        set_up, first_loaded = chip.sem("set_up"), chip.sem("first_loaded")
        pool_passed, cv_ready = chip.sem("pool_passed"), chip.sem("cv_ready")
        k_loaded2, y_free = chip.sem("k_loaded2"), chip.sem("y_free")
        k_loaded, k_hi, k_ready = chip.sem("k_loaded"), chip.sem("k_hi"), chip.sem("k_ready")
        v_loaded = [chip.sem(f"v_loaded{u}") for u in range(2)]
        v_hi, v_ready = chip.sem("v_hi"), chip.sem("v_ready")
        loaded = [chip.sem(f"loaded{u}") for u in range(2)]
        stored = [chip.sem(f"stored{u}") for u in range(2)]
        q_hi, q_ready = chip.sem("q_hi"), chip.sem("q_ready")
        unit_done, unit_free, chained, max_ready = (chip.sem(n) for n in ("unit_done", "unit_free", "chained", "max_ready"))
        scored, raised, split, probs_free = (chip.sem(n) for n in ("scored", "raised", "split", "probs_free"))
        passed = chip.sem("passed")
        odd_read, factored = chip.sem("odd_read"), chip.sem("factored")
        summed, inverted, y_done = chip.sem("summed"), chip.sem("inverted"), chip.sem("y_done")
        factor = inv_g if gamma else inv
        LOADS = 3 if channel else 2
        STORES = store.count

        def tiles(eng, step, peeled=(0, NT // 2 - 1, NT - 1)):
            def pair(b, r):
                for u in range(2):
                    step(b, 2 * r + u, r, u)

            r = 0
            while r < NT:
                if r in peeled:
                    pair(2 * r // NT, r)
                    r += 1
                else:
                    first, b = r, 2 * r // NT
                    while r not in peeled and 2 * r // NT == b:
                        r += 1
                    with eng.Fori(first, r) as at:
                        pair(b, at)

        def is_tile(tt, number):
            return isinstance(tt, int) and tt == number

        def batch_of_next(b, tt):
            return 1 if is_tile(tt, SWITCH) else b

        with nc.Block() as block:
            @block.sync
            def _(sp):
                def load(b, tt, u):
                    t = tt - b * NT
                    sp.dma_start(q_raw[:, u, :], q_dram[:, b, bass.ds(t * QT, QT)]).then_inc(loaded[u], 16)
                    sp.dma_start(x_in[:, u], x_dram[b, bass.ds(t * QT, QT), :].rearrange("(j p) c -> p j c", p=P)).then_inc(loaded[u], 16)
                    if channel:
                        sp.dma_start(cvT[:, u, :], channel[:, b, bass.ds(t * QT, QT)]).then_inc(loaded[u], 16)

                def step(b, tt, r, u):
                    if not is_tile(tt, 0):
                        sp.wait_ge(y_done, tt * SUB)
                        sp.sem_inc(passed, 1)
                    if not is_tile(tt, LAST):
                        load(batch_of_next(b, tt), tt + 1, 1 - u)
                    if not is_tile(tt, 0):
                        before = 0 if is_tile(tt, SWITCH + 1) else b
                        store(sp, before, tt - 1 - before * NT, y[:, 1 - u], stored[1 - u])
                    if not (is_tile(tt, 0) or is_tile(tt, 1)):
                        sp.wait_ge(stored[u], 16 * STORES * r)
                        sp.sem_inc(y_free, 1)

                sp.sem_inc(y_free, 2)
                sp.dma_start(k_raw[:], k_dram[:, 0, :]).then_inc(k_loaded, 16)
                load(0, 0, 0)
                load_first(sp, gam, mix if channel else None, first_loaded)
                tiles(sp, step, peeled=(0, NT // 2 - 1, NT // 2, NT - 1))
                sp.wait_ge(y_done, B * NT * SUB)
                store(sp, 1, NT - 1, y[:, 1], stored[1])
                for u in range(2):
                    sp.wait_ge(stored[u], 16 * STORES * (B * NT // 2))

            @block.tensor
            def _(pe):
                def unit(n, b, tt, u, r):
                    pe.wait_ge(unit_free, tt * NU + n + 1)
                    bank = 6 + n % 2
                    if units[n] == "max":
                        j, c = n // MC, n % MC
                        m = nc.tensor.matmul(psum[:, bank, :], Q[0:3 * D, u, j * P:(j + 1) * P],
                                             K[0:3 * D, b, c * BANK:(c + 1) * BANK], start=True, stop=True)
                    elif units[n] == "turn":
                        if n == NU - 2:
                            pe.wait_ge(chained, (tt + 1) * 4)
                        for j in (0, 1):
                            jj = 2 * (n - NU + 2) + j
                            m = nc.tensor.transpose(psum[0:2, bank, j * P:(j + 1) * P],
                                                    minus2[:, jj, :].bitcast(F32), chip.ident[:])
                    else:
                        j = n - MAXU
                        if j == 0:
                            pe.wait_ge(cv_ready, tt + 1)
                        m = nc.tensor.matmul(psum[:, bank, 0:C], CV[:, u, j * P:(j + 1) * P],
                                             MIX[:, b, :], start=True, stop=True)
                    m.then_inc(unit_done, 1)

                def scores(b, k, u):
                    nc.tensor.matmul(psum[:, 4 + k % 2, :], K[:, b, k * P:(k + 1) * P], Q[:, u, :],
                                     start=True, stop=True).then_inc(scored, 1)

                def step(b, tt, r, u):
                    nb, nu, nr = batch_of_next(b, tt), 1 - u, r + u
                    for k in range(MT):
                        n = tt * MT + k
                        ahead = (k + 2) % MT
                        if k + 2 < MT or not is_tile(tt, LAST):
                            if ahead == 0:
                                pe.wait_ge(max_ready, tt + 2)
                            pe.wait_ge(raised, n + 1)
                            scores(*((b, ahead, u) if k + 2 < MT else (nb, ahead, nu)))
                        if not is_tile(tt, LAST):
                            if unit_at[k] and unit_at[k][0] == 0:
                                if is_tile(tt, SWITCH):
                                    pe.wait_ge(k_ready, K_READY[1])
                                pe.wait_ge(q_ready, tt + 2)
                            for w in unit_at[k]:
                                unit(w, nb, tt + 1, nu, nr)
                        if k % VP == 0 and (b == 1 or is_tile(tt, 0)):
                            pe.wait_ge(v_ready, b * NP + k // VP + 1)
                        pe.wait_ge(split, n + 1)
                        for j in range(SUB):
                            part = slice(j * P, (j + 1) * P)
                            if k == 0:
                                if j % 2 == 0:
                                    wait(pe, y_done, (tt - 1) * SUB + j // 2 + 1)
                                else:
                                    wait(pe, odd_read, (tt - 1) * 2 + j // 2 + 1)
                            first, final = k == 0, k == MT - 1
                            nc.tensor.matmul(psum[:, j, 0:C + 2], e_hi[:, k % RING, part], V_hi[:, k, :],
                                             start=first, stop=False)
                            nc.tensor.matmul(psum[:, j, 0:C], e_hi[:, k % RING, part], V_lo[:, k, :],
                                             start=False, stop=False)
                            m = nc.tensor.matmul(psum[:, j, 0:C + 2], e_lo[:, k % RING, part], V_hi[:, k, :],
                                                 start=False, stop=final)
                            if final and j == 1:
                                m.then_inc(summed, 1)
                        m.then_inc(probs_free, 1)

                pe.sem_inc(probs_free, RING)
                pe.wait_ge(set_up, SET_UP)
                pe.wait_ge(k_ready, K_READY[0])
                pe.wait_ge(q_ready, 1)
                for w in range(NU):
                    unit(w, 0, 0, 0, 0)
                pe.wait_ge(max_ready, 1)
                scores(0, 0, 0)
                scores(0, 1, 0)
                tiles(pe, step)

            @block.scalar
            def _(act):
                def q_parts(r, u):
                    act.wait_ge(loaded[u], 16 * LOADS * (r + 1))
                    for at in (0, D):
                        nc.scalar.activation(Q[at:at + D, u, :], q_raw[:, u, :], ACT.Copy).then_inc(q_hi, 1)

                def v_part(b, p):
                    h, i = p // VL, p % VL
                    if i == 0:
                        act.wait_ge(v_loaded[h % 2], 16 * (b * (NP // VL // 2) + h // 2 + 1))
                    if b == 1:
                        act.wait_ge(probs_free, RING + SWITCH * MT + (p + 1) * VP)
                    nc.scalar.activation(V_hi[:, p * VP:(p + 1) * VP, 0:C], v_raw[:, h % 2, i * VP:(i + 1) * VP, :],
                                         ACT.Copy).then_inc(v_hi, 1)

                def odd_products(tt, u):
                    act.wait_ge(y_free, tt + 1)
                    for j in range(1, SUB, 2):
                        act.wait_ge(factored, 2 * tt + j // 2 + 1)
                        nc.scalar.activation(y[:, u, j, :], psum[:, j, 0:C], ACT.Copy,
                                             scale=factor[:, j:j + 1]).then_inc(odd_read, 1)

                def step(b, tt, r, u):
                    for k in range(MT):
                        n = tt * MT + k
                        if k == 2 and not is_tile(tt, 0):
                            odd_products(tt - 1, 1 - u)
                        if k == Q_AT and not is_tile(tt, LAST):
                            wait(act, scored, tt * MT)
                            q_parts(r + u, 1 - u)
                        act.wait_ge(scored, n + 1)
                        act.wait_ge(probs_free, n + 1)
                        nc.scalar.activation(e[:, k % RING, :], psum[:, 4 + k % 2, :], ACT.Exp, scale=scale)
                        nc.scalar.activation(e_hi[:, k % RING, :], psum[:, 4 + k % 2, :], ACT.Exp,
                                             scale=scale).then_inc(raised, 1)
                        if is_tile(tt, SWITCH) and k % VP == 0 and k >= 2 * VP:
                            v_part(1, k // VP - 2)
                    if is_tile(tt, SWITCH):
                        v_part(1, NP - 2)
                        v_part(1, NP - 1)

                act.wait_ge(k_loaded, 16)
                for at in (0, 2 * D):
                    nc.scalar.activation(K[at:at + D, 0, :], k_raw[:], ACT.Copy).then_inc(k_hi, 1)
                q_parts(0, 0)
                for p in range(NP):
                    v_part(0, p)
                tiles(act, step)
                odd_products(LAST, 1)

            @block.vector
            def _(dve):
                def q_low(tt, u):
                    dve.wait_ge(q_hi, 2 * tt + 2)
                    nc.vector.tensor_tensor(Q[2 * D:3 * D, u, :], q_raw[:, u, :], Q[0:D, u, :].bitcast(F32),
                                            ALU.subtract).then_inc(q_ready, 1)

                def unit(n, tt, u, r):
                    bank = 6 + n % 2
                    dve.wait_ge(unit_done, tt * NU + n + 1)
                    if units[n] == "max":
                        if n == 0:
                            wait(dve, chained, tt * 4)
                        j, c = n // MC, n % MC
                        nc.vector.tensor_reduce(tops[:, j, c:c + 1], psum[:, bank, :], AX.X, ALU.max).then_inc(unit_free, 1)
                        if n == MAXU - 1:
                            dve.wait_ge(unit_free, tt * NU + 2 + MAXU)
                            nc.vector.tensor_reduce(top[:], tops[:], AX.X, ALU.max).then_inc(chained, 1)
                            dve.wait_ge(chained, tt * 4 + 1)
                            nc.vector.tensor_scalar(minus[:, :, 0], top[:], -1.0, None, ALU.mult).then_inc(chained, 1)
                            dve.wait_ge(chained, tt * 4 + 2)
                            nc.vector.tensor_copy(minus2[:, :, 0:1], minus[:]).then_inc(chained, 1)
                            dve.wait_ge(chained, tt * 4 + 3)
                            nc.vector.tensor_tensor(minus2[:, :, 1:2], minus[:], minus2[:, :, 0:1].bitcast(F32),
                                                    ALU.subtract).then_inc(chained, 1)
                    elif units[n] == "turn":
                        h = n - (NU - 2)
                        nc.vector.tensor_copy(Q[3 * D:3 * D + 2, u, h * 2 * P:(h + 1) * 2 * P],
                                              psum[0:2, bank, 0:2 * P]).then_inc(unit_free, 1)
                        if h == 1:
                            dve.wait_ge(unit_free, tt * NU + 2 + n + 1)
                            nc.vector.sem_inc(max_ready, 1)
                    else:
                        j = n - MAXU
                        if j == 0:
                            dve.wait_ge(loaded[u], 16 * LOADS * (r + 1))
                        nc.vector.tensor_tensor(x_in[:, u, j, :], psum[:, bank, 0:C], x_in[:, u, j, :],
                                                ALU.add).then_inc(unit_free, 1)

                def finish(tt, r, u):
                    dve.wait_ge(loaded[u], 16 * LOADS * (r + 1))
                    dve.wait_ge(y_free, tt + 1)
                    if channel:
                        dve.wait_ge(unit_free, (tt + 1) * NU + 2)
                    for j in range(0, SUB, 2):
                        if j == 0:
                            dve.wait_ge(summed, tt + 1)
                        else:
                            dve.wait_ge(probs_free, RING + (tt + 1) * MT)
                        wait(dve, y_done, tt * SUB)
                        wait(dve, odd_read, (tt - 1) * 2 + j // 2 + 1)
                        nc.vector.reciprocal(inv[:, j:j + 2, None], psum[:, j:j + 2, C:C + 1]).then_inc(inverted, 1)
                        dve.wait_ge(inverted, 2 * tt + j // 2 + 1)
                        if gamma:
                            nc.vector.tensor_scalar(inv_g[:, j:j + 2], inv[:, j:j + 2], gam[:], None, ALU.mult)
                            dve.drain()
                        nc.vector.sem_inc(factored, 1)
                        nc.vector.scalar_tensor_tensor(out=y[:, u, j, :], in0=psum[:, j, 0:C], scalar=factor[:, j:j + 1],
                                                       in1=x_in[:, u, j, :], op0=ALU.mult, op1=ALU.add).then_inc(y_done, 1)
                    for j in range(1, SUB, 2):
                        dve.wait_ge(odd_read, 2 * tt + j // 2 + 1)
                        nc.vector.tensor_tensor(y[:, u, j, :], y[:, u, j, :], x_in[:, u, j, :], ALU.add).then_inc(y_done, 1)

                def step(b, tt, r, u):
                    for k in range(MT):
                        n = tt * MT + k
                        dve.wait_ge(raised, n + 1)
                        dve.wait_ge(probs_free, n + 1)
                        nc.vector.tensor_tensor(e_lo[:, k % RING, :], e[:, k % RING, :],
                                                e_hi[:, k % RING, :].bitcast(F32), ALU.subtract).then_inc(split, 1)
                        if k == 0 and not is_tile(tt, 0):
                            finish(tt - 1, r - 1 + u, 1 - u)
                        if not is_tile(tt, LAST):
                            if k == Q_AT:
                                q_low(tt + 1, 1 - u)
                            for w in unit_at[k - 1] if k else ():
                                unit(w, tt + 1, 1 - u, r + u)

                nc.vector.memset(K[3 * D:3 * D + 2, :, :].bitcast(F32), 1.0).then_inc(set_up, 1)
                nc.vector.memset(V_hi[:, :, C:C + 1].bitcast(F32), 1.0).then_inc(set_up, 1)
                nc.vector.memset(V_hi[:, :, C + 1:C + 2].bitcast(F32), 0.0).then_inc(set_up, 1)
                nc.vector.memset(top[:], 0.0).then_inc(set_up, 1)
                nc.vector.sem_inc(unit_free, 2)
                dve.wait_ge(k_hi, 2)
                nc.vector.tensor_tensor(K[D:2 * D, 0, :], k_raw[:], K[0:D, 0, :].bitcast(F32),
                                        ALU.subtract).then_inc(k_ready, 1)
                q_low(0, 0)
                dve.wait_ge(first_loaded, 16 * load_first.count)
                for w in range(NU):
                    unit(w, 0, 0, 0)
                tiles(dve, step)
                finish(LAST, NT - 1, 1)

            @block.gpsimd
            def _(pool):
                def load_v(b, h):
                    if b == 1 or h >= 2:
                        pool.wait_ge(v_ready, b * NP + (h - 1) * VL)
                    at = slice(h * VL * VP * P, (h + 1) * VL * VP * P)
                    pool.dma_start(v_raw[:, h % 2], v_dram[b, at].rearrange("(m p) c -> p m c", p=P)).then_inc(v_loaded[h % 2], 16)

                def v_low(b, p):
                    pool.wait_ge(v_hi, b * NP + p + 1)
                    h, i, at = p // VL, p % VL, slice(p * VP, (p + 1) * VP)
                    nc.gpsimd.tensor_tensor(V_lo[:, at, :], v_raw[:, h % 2, i * VP:(i + 1) * VP, :],
                                            V_hi[:, at, 0:C].bitcast(F32), ALU.subtract).then_inc(v_ready, 1)

                def parts(dst, src, low_at):
                    for at in (0, 2 * D if low_at == D else D):
                        nc.gpsimd.tensor_copy(dst[at:at + D], src)
                        pool.drain()
                    return nc.gpsimd.tensor_tensor(dst[low_at:low_at + D], src, dst[0:D].bitcast(F32), ALU.subtract)

                def channel_parts(tt, r, u):
                    pool.wait_ge(loaded[u], 16 * LOADS * (r + 1))
                    wait(pool, unit_done, (tt - 1) * NU)
                    pool.sem_inc(pool_passed, 1)
                    parts(CV[:, u], cvT[:, u], 2 * D).then_inc(cv_ready, 1)
                    pool.drain()

                def step(b, tt, r, u):
                    if is_tile(tt, 1):
                        pool.wait_ge(k_ready, K_READY[0])
                        pool.dma_start(k_raw[:], k_dram[:, 1, :]).then_inc(k_loaded2, 16)
                        load_v(1, 0)
                        load_v(1, 1)
                    if channel and not is_tile(tt, LAST):
                        channel_parts(tt + 1, r + u, 1 - u)
                    if is_tile(tt, SWITCH - 1):
                        pool.wait_ge(k_loaded2, 16)
                        for c in range(0, HW, K_PIECE):
                            parts(K[0:3 * D, 1, c:c + K_PIECE], k_raw[:, c:c + K_PIECE], D).then_inc(k_ready, 1)
                            pool.drain()
                    if is_tile(tt, SWITCH):
                        split_v(1)

                def split_v(b):
                    for p in range(NP):
                        v_low(b, p)
                        if p % VL == VL - 1 and p // VL + 2 < NP // VL:
                            load_v(b, p // VL + 2)

                load_v(0, 0)
                load_v(0, 1)
                if channel:
                    pool.wait_ge(first_loaded, 16 * load_first.count)
                    for b in range(B):
                        parts(MIX[:, b], mix[:, b], D)
                        pool.drain()
                    channel_parts(0, 0, 0)
                split_v(0)
                tiles(pool, step)


CR = 16
TILES = T // P
TB = HW // P


def project2(nc, chip, x2_dram, wq, bq, wk, bk, wv, bv, wcq, bcq, wck, bck, wcv, bcv, wp, bp,
             qkc_dram, v_dram, mix_dram):
    chip.part = "project2"
    psum = chip.psum
    CV = C + 2 * CR
    SLOTS = 4
    with ExitStack() as ctx:
        def sb(name, shape, dt=F32):
            return ctx.enter_context(nc.sbuf_tensor("p2_" + name, shape, dt))

        w_t, w_m = sb("w_t", [P, KC, 3 * D]), sb("w_m", [P, KC, CV])
        b_t, b_m = sb("b_t", [3 * D, 1]), sb("b_m", [P, CV])
        wp_sb = sb("wp", [CR, C])
        x_in, xT = sb("x_in", [P, SLOTS, C]), sb("xT", [P, 2, KC, P])
        t_out, v_out = sb("t_out", [3 * D, SLOTS, P]), sb("v_out", [P, SLOTS, C])
        cqk = sb("cqk", [P, TILES, 2 * CR])
        top, low, total, inv = (sb(n, [CR, B]) for n in ("top", "low", "total", "inv"))
        ex, attn = sb("ex", [CR, B, CR]), sb("attn", [CR, B, CR])
        mix = sb("mix", [D, B, C])

        cleared, weights, mix_loaded = chip.sem("cleared"), chip.sem("weights"), chip.sem("mix_loaded")
        loaded = [chip.sem(f"loaded{u}") for u in range(SLOTS)]
        stored = [chip.sem(f"stored{u}") for u in range(SLOTS)]
        transposed, xT_copied, t_done, t_copied, v_done, v_copied = (chip.sem(n) for n in (
            "transposed", "xT_copied", "t_done", "t_copied", "v_done", "v_copied"))
        scored, steps, raised, mixed, mix_stored = (chip.sem(n) for n in ("scored", "steps", "raised", "mixed", "mix_stored"))
        NW = 6 + 6 + 1

        with nc.Block() as block:
            @block.sync
            def _(sp):
                def load(s, u):
                    sp.dma_start(x_in[:, u, :], x2_dram[bass.ds(s * P, P), :]).then_inc(loaded[u], 16)

                def step(s, r, u, more=True):
                    if more:
                        sp.wait_ge(transposed, s + 1)
                        load(s + SLOTS, u)
                    sp.wait_ge(t_copied, s + 1)
                    sp.dma_start(qkc_dram[:, bass.ds(s * P, P)], t_out[:, u, :]).then_inc(stored[u], 16)
                    sp.wait_ge(v_copied, 2 * s + 1)
                    sp.dma_start(v_dram[bass.ds(s * P, P), :], v_out[:, u, :]).then_inc(stored[u], 16)

                for u in range(SLOTS):
                    load(u, u)
                sp.wait_ge(cleared, 5)
                for at, w, b in ((0, wq, bq), (D, wk, bk), (2 * D, wcv, bcv)):
                    sp.dma_start(w_t[:, :, at:at + CR], rows(w)).then_inc(weights, 16)
                    sp.dma_start(b_t[at:at + CR, :], column(b)).then_inc(weights, 16)
                for at, w, b in ((0, wv, bv), (C, wcq, bcq), (C + CR, wck, bck)):
                    n = w.shape[1]
                    sp.dma_start(w_m[:, :, at:at + n], rows(w)).then_inc(weights, 16)
                    sp.dma_start(b_m[:, at:at + n], across(b)).then_inc(weights, 16)
                sp.dma_start(wp_sb[:], wp).then_inc(weights, 16)
                for b in range(B):
                    sp.dma_start(mix[CR:CR + 1, b, :], across(bp, 1)).then_inc(mix_loaded, 16)
                with sp.Fori(0, TILES // SLOTS - 1) as r:
                    for u in range(SLOTS):
                        step(r * SLOTS + u, r, u)
                for u in range(SLOTS):
                    step(TILES - SLOTS + u, TILES // SLOTS - 1, u, more=False)
                sp.wait_ge(mix_loaded, 16 * B)
                sp.wait_ge(steps, 5)
                sp.dma_start(mix_dram, mix[:]).then_inc(mix_stored, 16)
                for u in range(SLOTS):
                    sp.wait_ge(stored[u], 2 * 16 * (TILES // SLOTS))
                sp.wait_ge(mix_stored, 16)

            @block.tensor
            def _(pe):
                def transposes(s, r, u):
                    pe.wait_ge(loaded[u], 16 * (r + 1))
                    wait(pe, xT_copied, s - 1)
                    for k in range(KC):
                        m = nc.tensor.transpose(psum[:, u % 2, k * P:(k + 1) * P], x_in[:, u, k * P:(k + 1) * P],
                                                chip.ident[:])
                    m.then_inc(transposed, 1)

                def step(s, r, u):
                    if not (isinstance(s, int) and s == TILES - 1):
                        transposes(s + 1, r + (u + 1) // SLOTS, (u + 1) % SLOTS)
                    pe.wait_ge(xT_copied, s + 1)
                    wait(pe, t_copied, s - 1)
                    for k in range(KC):
                        m = nc.tensor.matmul(psum[0:3 * D, 2 + u % 2, 0:P], w_t[:, k, :], xT[:, u % 2, k, :],
                                             start=(k == 0), stop=(k == KC - 1))
                    m.then_inc(t_done, 1)
                    wait(pe, v_copied, 2 * (s - 1))
                    for k in range(KC):
                        m = nc.tensor.matmul(psum[:, 4 + u % 2, 0:CV], xT[:, u % 2, k, :], w_m[:, k, :],
                                             start=(k == 0), stop=(k == KC - 1))
                    m.then_inc(v_done, 1)

                pe.wait_ge(weights, 16 * NW)
                transposes(0, 0, 0)
                turns(pe, TILES, step, unroll=SLOTS)
                pe.wait_ge(v_copied, 2 * TILES)
                for b in range(B):
                    for s in range(TB):
                        m = nc.tensor.matmul(psum[0:CR, 6, b * CR:(b + 1) * CR], cqk[:, b * TB + s, CR:2 * CR],
                                             cqk[:, b * TB + s, 0:CR], start=(s == 0), stop=(s == TB - 1))
                m.then_inc(scored, 1)
                pe.wait_ge(steps, 4)
                for b in range(B):
                    m = nc.tensor.matmul(psum[0:CR, 7, b * C:(b + 1) * C], attn[:, b, :], wp_sb[:],
                                         start=True, stop=True)
                m.then_inc(mixed, 1)

            @block.scalar
            def _(act):
                def step(s, r, u):
                    act.wait_ge(transposed, s + 1)
                    wait(act, v_done, s - 1)
                    nc.scalar.activation(xT[:, u % 2], psum[:, u % 2, 0:C].rearrange("p (k n) -> p k n", k=KC),
                                         ACT.Copy).then_inc(xT_copied, 1)
                    act.wait_ge(t_done, s + 1)
                    wait(act, stored[u], 2 * 16 * r)
                    nc.scalar.activation(t_out[:, u, :], psum[0:3 * D, 2 + u % 2, 0:P], ACT.Identity,
                                         bias=b_t[:]).then_inc(t_copied, 1)

                act.wait_ge(weights, 16 * NW)
                turns(act, TILES, step, unroll=SLOTS)
                act.wait_ge(steps, 2)
                for b in range(B):
                    nc.scalar.activation(ex[:, b, :], psum[0:CR, 6, b * CR:(b + 1) * CR], ACT.Exp, bias=low[:, b:b + 1],
                                         scale=float(CR) ** -0.5, accum_out=total[:, b:b + 1]).then_inc(raised, 1)

            @block.vector
            def _(dve):
                def step(s, r, u):
                    dve.wait_ge(v_done, s + 1)
                    wait(dve, stored[u], 2 * 16 * r)
                    nc.vector.tensor_tensor(v_out[:, u, :], psum[:, 4 + u % 2, 0:C], b_m[:, 0:C], ALU.add).then_inc(v_copied, 1)
                    nc.vector.tensor_tensor(cqk[:, s, :], psum[:, 4 + u % 2, C:CV], b_m[:, C:CV], ALU.add).then_inc(v_copied, 1)

                nc.vector.memset(w_t[:], 0.0).then_inc(cleared, 1)
                nc.vector.memset(b_t[0:2 * D, :], 0.0).then_inc(cleared, 1)
                nc.vector.memset(b_t[2 * D:3 * D, :], 1.0).then_inc(cleared, 1)
                nc.vector.memset(mix[:], 0.0).then_inc(cleared, 1)
                nc.vector.memset(total[:], 0.0).then_inc(cleared, 1)
                dve.wait_ge(weights, 16 * NW)
                turns(dve, TILES, step, unroll=SLOTS)
                dve.wait_ge(scored, 1)
                nc.vector.tensor_reduce(top[:], psum[0:CR, 6, 0:B * CR].rearrange("p (b n) -> p b n", b=B),
                                        AX.X, ALU.max).then_inc(steps, 1)
                dve.wait_ge(steps, 1)
                nc.vector.tensor_scalar(low[:], top[:], -float(CR) ** -0.5, None, ALU.mult).then_inc(steps, 1)
                dve.wait_ge(raised, B)
                nc.vector.reciprocal(inv[:], total[:]).then_inc(steps, 1)
                dve.wait_ge(steps, 3)
                nc.vector.tensor_tensor(attn[:], ex[:], inv[:, :, None].broadcast_to([CR, B, CR]), ALU.mult).then_inc(steps, 1)
                dve.wait_ge(mixed, 1)
                nc.vector.tensor_copy(mix[0:CR, :, :], psum[0:CR, 7, :].rearrange("p (b c) -> p b c", b=B)).then_inc(steps, 1)


S1 = N + 1
S2 = N + 2


def clear_borders(nc, chip, corners_dram, padded_dram):
    chip.part = "borders"
    zeros_ready, stored = chip.sem("zeros_ready"), chip.sem("stored")
    with nc.sbuf_tensor("zeros", [S2, 2 * C], F32) as zeros, nc.Block() as block:
        @block.gpsimd
        def _(pool):
            nc.gpsimd.memset(zeros[:], 0.0).then_inc(zeros_ready, 1)

        @block.sync
        def _(sp):
            sp.wait_ge(zeros_ready, 1)
            count = 0
            for b in range(B):
                at = corners_dram[b]
                for dst in (at[0, :, 0:2, :], at[S1 - 1, :, 2:4, :]):
                    sp.dma_start(dst.rearrange("x k c -> x (k c)"), zeros[0:S1, :]).then_inc(stored, 16)
                    count += 1
                for dst in (at[1:S1, 0, 0, :], at[0:S1 - 1, 0, 2, :], at[1:S1, S1 - 1, 1, :], at[0:S1 - 1, S1 - 1, 3, :]):
                    sp.dma_start(dst, zeros[0:N, 0:C]).then_inc(stored, 16)
                    count += 1
                pad = padded_dram[b]
                for dst, n in ((pad[0], S2), (pad[S2 - 1], S2), (pad[1:S2 - 1, 0], N), (pad[1:S2 - 1, S2 - 1], N)):
                    sp.dma_start(dst, zeros[0:n, 0:C]).then_inc(stored, 16)
                    count += 1
            sp.wait_ge(stored, 16 * count)


def corner_store(corners_dram, padded_dram):
    def store(sp, b, t, y_slot, sem):
        for h in range(2):
            half = y_slot[h * N:(h + 1) * N]
            sp.dma_start(padded_dram[b, bass.ds(t * (QT // N) + h + 1, SUB, 2), 1:N + 1, :].rearrange("j x c -> x j c"),
                         half).then_inc(sem, 16)
            for dy in range(2):
                for dx in range(2):
                    sp.dma_start(corners_dram[b, bass.ds(t * (QT // N) + h + 1 - dy, SUB, 2), 1 - dx:N + 1 - dx,
                                              2 * dy + dx, :].rearrange("j x c -> x j c"), half).then_inc(sem, 16)

    store.count = 2 * (1 + 4)
    return store


TAPS = 9
OFF = 3 * TAPS
OQ = 32
GROUPS = P // OQ
YT = 8
YTOK = YT * N
SPAN_ROWS = (YT + 2) * S2
FULL = SPAN_ROWS // P
REST = SPAN_ROWS - FULL * P


def offsets(nc, chip, padded_dram, offset_w, off_all, load_more):
    chip.part = "offsets"
    psum = chip.psum
    OT = B * N // YT
    with ExitStack() as ctx:
        def sb(name, shape, dt=F32):
            return ctx.enter_context(nc.sbuf_tensor("off_" + name, shape, dt))

        w = sb("w", [P, TAPS, KC, OQ])
        stack = sb("stack", [P, OQ])
        x_in = sb("x_in", [P, 2, FULL + 1, C])
        xT = sb("xT", [P, 2, KC, SPAN_ROWS])
        oT = sb("oT", [P, 2, YTOK])
        cleared, weights = chip.sem("cleared"), chip.sem("weights")
        loaded = [chip.sem(f"loaded{u}") for u in range(2)]
        turned, xT_copied, xT2_copied, convolved, oT_copied, added, kept = (chip.sem(n) for n in (
            "turned", "xT_copied", "xT2_copied", "convolved", "oT_copied", "added", "kept"))

        with nc.Block() as block:
            @block.sync
            def _(sp):
                def load(b, yt, u):
                    rows_at = padded_dram[b].rearrange("y x c -> (y x) c")
                    sp.dma_start(x_in[:, u, 0:FULL, :], rows_at[bass.ds(yt * (YT * S2), FULL * P), :]
                                 .rearrange("(i p) c -> p i c", p=P)).then_inc(loaded[u], 16)
                    sp.dma_start(x_in[0:REST, u, FULL, :], rows_at[bass.ds(yt * (YT * S2) + FULL * P, REST), :]
                                 ).then_inc(loaded[u], 16)

                sp.wait_ge(cleared, 1)
                sp.dma_start(w[:, :, :, 0:OFF], offset_w.rearrange("a b (k p) f -> p (a b) k f", p=P)).then_inc(weights, 16)
                load(0, 0, 0)
                load(0, 1, 1)
                load_more(sp)
                with sp.Fori(1, OT // 2 // B) as r:
                    for u in range(2):
                        sp.wait_ge(turned, r * 2 + u - 1)
                        load(0, r * 2 + u, u)
                with sp.Fori(0, OT // 2 // B) as r:
                    for u in range(2):
                        sp.wait_ge(turned, r * 2 + u + OT // B - 1)
                        load(1, r * 2 + u, u)

            @block.tensor
            def _(pe):
                def turn(s, r, u):
                    pe.wait_ge(loaded[u], 32 * (r + 1))
                    for k in range(KC):
                        wait(pe, (xT_copied, xT2_copied)[k], s)
                        for i in range(FULL + 1):
                            n = P if i < FULL else REST
                            m = nc.tensor.transpose(psum[:, 2 * k + i // 4, (i % 4) * P:(i % 4) * P + n],
                                                    x_in[0:n, u, i, k * P:(k + 1) * P], chip.ident[0:n, 0:n])
                    m.then_inc(turned, 1)

                def step(s, r, u):
                    if not (isinstance(s, int) and s == OT - 1):
                        turn(s + 1, r + u, 1 - u)
                    pe.wait_ge(xT_copied, s + 1)
                    pe.wait_ge(xT2_copied, s + 1)
                    wait(pe, oT_copied, s - 1)
                    for n in range(TAPS * KC):
                        tap, k, q = n // KC, n % KC, n % GROUPS
                        view = xT[:, u, k, :].rearrange("p (y x) -> p y x", x=S2)[:, tap // 3:tap // 3 + YT, tap % 3:tap % 3 + N]
                        m = nc.tensor.matmul(psum[q * OQ:(q + 1) * OQ, 4 + u, :], w[:, tap, k, :], view,
                                             start=(n < GROUPS), stop=(n >= TAPS * KC - GROUPS), tile_position=(0, q * OQ))
                    m.then_inc(convolved, 1)
                    if not (isinstance(s, int) and s == 0):
                        add(s - 1, 1 - u)

                def add(s, u):
                    pe.wait_ge(oT_copied, s + 1)
                    wait(pe, kept, s - 1)
                    for j in range(YTOK // P):
                        m = nc.tensor.matmul(psum[:, 6 + u, j * OQ:(j + 1) * OQ], oT[:, u, j * P:(j + 1) * P], stack[:],
                                             start=True, stop=True)
                    m.then_inc(added, 1)

                pe.wait_ge(weights, 16)
                turn(0, 0, 0)
                turns(pe, OT, step, head=2)
                add(OT - 1, 1)

            def x_copy(copy, eng, done, k, s, u):
                eng.wait_ge(turned, s + 1)
                wait(eng, convolved, s - 1)
                copy(xT[:, u, k, :], psum[:, 2 * k:2 * k + 2, :].rearrange("p a n -> p (a n)")[:, 0:SPAN_ROWS]).then_inc(done, 1)

            @block.scalar
            def _(act):
                def copy(dst, src):
                    return nc.scalar.activation(dst, src, ACT.Copy)

                def step(s, r, u):
                    if not (isinstance(s, int) and s == OT - 1):
                        x_copy(copy, act, xT_copied, 0, s + 1, 1 - u)
                    act.wait_ge(convolved, s + 1)
                    wait(act, added, s - 1)
                    copy(oT[:, u, :], psum[:, 4 + u, :]).then_inc(oT_copied, 1)

                x_copy(copy, act, xT_copied, 0, 0, 0)
                turns(act, OT, step)

            @block.vector
            def _(dve):
                def step(s, r, u):
                    if not (isinstance(s, int) and s == OT - 1):
                        x_copy(nc.vector.tensor_copy, dve, xT2_copied, 1, s + 1, 1 - u)
                    if not (isinstance(s, int) and s == 0):
                        keep(s - 1, 1 - u)

                def keep(s, u):
                    dve.wait_ge(added, s + 1)
                    per = YTOK // P
                    nc.vector.tensor_scalar(off_all[:, bass.ds(s * per, per), :],
                                            psum[:, 6 + u, 0:per * OQ].rearrange("p (j f) -> p j f", f=OQ), 1.0, None,
                                            ALU.mult).then_inc(kept, 1)

                nc.vector.memset(w[:], 0.0).then_inc(cleared, 1)
                nc.vector.tensor_reduce(stack[:], chip.ident[:].rearrange("p (q f) -> p f q", q=GROUPS), AX.X, ALU.add)
                x_copy(nc.vector.tensor_copy, dve, xT2_copied, 1, 0, 0)
                turns(dve, OT, step, head=2)
                keep(OT - 1, 1)


def sample_plan(nc, chip, off_all, place, weight):
    chip.part = "plan"
    with ExitStack() as ctx:
        def sb(name, shape, dt=F32):
            return ctx.enter_context(nc.sbuf_tensor("plan_" + name, shape, dt))

        A = 2 * TAPS
        grid_i, grid = sb("grid_i", [P, TILES, A], I32), sb("grid", [P, TILES, A])
        whole_i = sb("whole_i", [P, TILES, A], I32)
        pos, base, above, held = (sb(n, [P, TILES, A]) for n in ("pos", "base", "above", "held"))
        w1, w0 = sb("w1", [P, TILES, A]), sb("w0", [P, TILES, A])
        mask = sb("mask", [P, TILES, TAPS])
        grid_ready, mask_ready = chip.sem("grid_ready"), chip.sem("mask_ready")

        with nc.Block() as block:
            @block.gpsimd
            def _(pool):
                for h in range(2):
                    half = slice(h * N, (h + 1) * N)
                    for b in range(B):
                        span = slice(b * (TILES // B), (b + 1) * (TILES // B))
                        nc.gpsimd.iota(grid_i[half, span, 0:TAPS], pattern=[[2, TILES // B], [1, 3], [0, 3]], base=h - 1,
                                       channel_multiplier=0)
                    nc.gpsimd.iota(grid_i[half, :, TAPS:A], pattern=[[0, TILES], [0, 3], [1, 3]], base=-1,
                                   channel_multiplier=1)
                nc.gpsimd.drain()
                nc.gpsimd.tensor_copy(grid[:], grid_i[:]).then_inc(grid_ready, 1)

            @block.scalar
            def _(act):
                nc.scalar.activation(mask[:], off_all[:, :, A:OFF], ACT.Sigmoid).then_inc(mask_ready, 1)

            @block.vector
            def _(dve):
                y, x = slice(0, TAPS), slice(TAPS, A)
                dve.wait_ge(grid_ready, 1)
                nc.vector.tensor_tensor(pos[:], off_all[:, :, 0:A], grid[:], ALU.add)
                dve.drain()
                nc.vector.tensor_scalar(pos[:], pos[:], -2.0, float(N + 1), ALU.max, ALU.min)
                dve.drain()
                nc.vector.tensor_copy(whole_i[:], pos[:])
                dve.drain()
                nc.vector.tensor_copy(base[:], whole_i[:])
                dve.drain()
                nc.vector.tensor_tensor(above[:], base[:], pos[:], ALU.is_gt)
                dve.drain()
                nc.vector.tensor_tensor(base[:], base[:], above[:], ALU.subtract)
                dve.drain()
                nc.vector.tensor_tensor(w1[:], pos[:], base[:], ALU.subtract)
                nc.vector.tensor_scalar(held[:], base[:], -1.0, float(N - 1), ALU.max, ALU.min)
                dve.drain()
                nc.vector.tensor_scalar(w0[:], w1[:], -1.0, 1.0, ALU.mult, ALU.add)
                nc.vector.tensor_tensor(above[:], base[:], held[:], ALU.is_equal)
                dve.drain()
                nc.vector.tensor_tensor(w1[:], w1[:], above[:], ALU.mult)
                nc.vector.tensor_tensor(w0[:], w0[:], above[:], ALU.mult)
                nc.vector.scalar_tensor_tensor(out=pos[:, :, y], in0=held[:, :, y], scalar=float(S1), in1=held[:, :, x],
                                               op0=ALU.mult, op1=ALU.add)
                dve.drain()
                dve.wait_ge(mask_ready, 1)
                for w in (w0, w1):
                    nc.vector.tensor_tensor(w[:, :, y], w[:, :, y], mask[:], ALU.mult)
                for b in range(B):
                    span = slice(b * (TILES // B), (b + 1) * (TILES // B))
                    nc.vector.tensor_scalar(place[:, span, :], pos[:, span, y], float(S1 + 1 + b * S1 * S1), None, ALU.add)
                dve.drain()
                for dy, wy in enumerate((w0, w1)):
                    for dx, wx in enumerate((w0, w1)):
                        nc.vector.tensor_tensor(weight[:, :, :, 2 * dy + dx], wy[:, :, y], wx[:, :, x], ALU.mult)
                dve.drain()


class SamplingConstants:

    def __init__(self, nc, chip, ctx, dcn_w, gamma, beta, mean, var):
        def sb(name, shape):
            return ctx.enter_context(nc.sbuf_tensor("dcn_" + name, shape, F32))

        chip.part = "dcn_constants"
        self.w = sb("w", [P, TAPS, KC, C])
        self.mean, self.gamma, self.beta, self.root = (sb(n, [P, C]) for n in ("mean", "gamma", "beta", "root"))
        self.loaded, self.count = chip.sem("loaded"), 16 * 5
        self.sources = (dcn_w, mean, gamma, beta, var)

    def load(self, sp):
        dcn_w, *vectors = self.sources
        sp.dma_start(self.w[:], dcn_w.rearrange("a b (k p) f -> p (a b) k f", p=P)).then_inc(self.loaded, 16)
        for dst, v in zip((self.mean, self.gamma, self.beta, self.root), vectors):
            sp.dma_start(dst[:], across(v)).then_inc(self.loaded, 16)


def deformable(nc, chip, corners_dram, constants, place, weight, out):
    chip.part = "dcn"
    psum = chip.psum
    R = 3
    with ExitStack() as ctx:
        def sb(name, shape, dt=F32):
            return ctx.enter_context(nc.sbuf_tensor("dcn_" + name, shape, dt))

        w, mean_r, gamma_r, beta_r, std_r = constants.w, constants.mean, constants.gamma, constants.beta, constants.root
        pix = sb("pix", [P, 2, TAPS, 4 * C])
        at, part = sb("at", [P, 2, TAPS], I32), sb("part", [P, 2, TAPS, 4])
        blend = sb("blend", [P, R, C])
        bT = sb("bT", [P, 2, KC, P])
        inv_r = sb("inv_r", [P, C])
        eps = sb("eps", [P, 1])
        y1, y2, y = sb("y1", [P, 2, C]), sb("y2", [P, 2, C]), sb("y", [P, 2, C])

        weights = constants.loaded
        eps_set, rooted, norm_ready, staged = (chip.sem(n) for n in ("eps_set", "rooted", "norm_ready", "staged"))
        passed = chip.sem("passed")
        gathered = [[chip.sem(f"gathered{u}_{t}") for t in range(TAPS)] for u in range(2)]
        first_corner, blended, turned, bT_copied, multiplied = (chip.sem(n) for n in (
            "first_corner", "blended", "turned", "bT_copied", "multiplied"))
        centred, scaled, finished = chip.sem("centred"), chip.sem("scaled"), chip.sem("finished")
        stored = [chip.sem(f"stored{u}") for u in range(2)]
        table = corners_dram.rearrange("b y x k c -> (b y x) (k c)")
        out_rows = out.rearrange("b y x c -> (b y x) c")
        last = 2 * TAPS - 1

        with nc.Block() as block:
            @block.sync
            def _(sp):
                with sp.Fori(0, TILES // 2) as r:
                    for u in range(2):
                        s = r * 2 + u
                        sp.wait_ge(finished, s + 1)
                        sp.dma_start(out_rows[bass.ds(s * P, P), :], y[:, u, :]).then_inc(stored[u], 16)
                for u in range(2):
                    sp.wait_ge(stored[u], 16 * (TILES // 2))

            @block.gpsimd
            def _(pool):
                def gather(s, r, u):
                    pool.wait_ge(staged, s + 1)
                    pool.sem_inc(passed, 1)
                    for t in range(TAPS):
                        wait(pool, blended, (s - 2) * TAPS + t + 1)
                        if not isinstance(s, int) or s >= 2:
                            pool.sem_inc(passed, 1)
                        nc.gpsimd.indirect_dma_start(pix[:, u, t, :], None, table, bass.IndirectOffsetOnAxis(
                            at[:, u, t:t + 1], 0)).then_inc(gathered[u][t], 16)

                def finish(s, r, u):
                    pool.wait_ge(centred, s + 1)
                    wait(pool, finished, s - 1)
                    nc.gpsimd.tensor_tensor(y2[:, u, :], y1[:, u, :], inv_r[:], ALU.mult).then_inc(scaled, 1)
                    pool.wait_ge(scaled, 2 * s + 1)
                    nc.gpsimd.tensor_tensor(y2[:, u, :], y2[:, u, :], beta_r[:], ALU.add).then_inc(scaled, 1)

                def step(s, r, u):
                    if not (isinstance(s, int) and s == TILES - 1):
                        gather(s + 1, r + u, 1 - u)
                    finish(s, r, u)

                gather(0, 0, 0)
                pool.wait_ge(norm_ready, 2)
                pool.wait_ge(weights, constants.count)
                turns(pool, TILES, step, head=2)

            @block.vector
            def _(dve):
                def stage(s, u):
                    wait(dve, first_corner, (s - 1) * TAPS)
                    nc.vector.tensor_scalar(at[:, u, :], place[:, s, :], 1.0, None, ALU.mult)
                    nc.vector.tensor_scalar(part[:, u], weight[:, s], 1.0, None, ALU.mult).then_inc(staged, 1)

                def finish(s, u):
                    dve.wait_ge(multiplied, TAPS * (s + 1))
                    wait(dve, scaled, 2 * (s - 1))
                    nc.vector.tensor_tensor(y1[:, u, :], psum[:, 4 + u, 0:C], mean_r[:], ALU.subtract).then_inc(centred, 1)

                def step(s, r, u):
                    for t in range(TAPS):
                        n, slot = s * TAPS + t, (u * TAPS + t) % R
                        if t == 2:
                            if not (isinstance(s, int) and s == 0):
                                finish(s - 1, 1 - u)
                        dve.wait_ge(gathered[u][t], 16 * (r + 1))
                        dve.wait_ge(first_corner, n + 1)
                        for k in range(1, 4):
                            m = nc.vector.scalar_tensor_tensor(
                                out=blend[:, slot, :], in0=pix[:, u, t, k * C:(k + 1) * C], scalar=part[:, u, t, k:k + 1],
                                in1=blend[:, slot, :], op0=ALU.mult, op1=ALU.add)
                            if k < 3:
                                dve.drain()
                        m.then_inc(blended, 1)
                        if t == 0 and not (isinstance(s, int) and s == TILES - 1):
                            stage(s + 1, 1 - u)

                nc.vector.memset(eps[:], 1e-3).then_inc(eps_set, 1)
                dve.wait_ge(rooted, 1)
                nc.vector.reciprocal(inv_r[:], std_r[:]).then_inc(norm_ready, 1)
                dve.wait_ge(norm_ready, 1)
                nc.vector.tensor_tensor(inv_r[:], inv_r[:], gamma_r[:], ALU.mult).then_inc(norm_ready, 1)
                stage(0, 0)
                turns(dve, TILES, step, head=2)
                finish(TILES - 1, 1)

            @block.scalar
            def _(act):
                def first(s, r, u, t):
                    n, slot = s * TAPS + t, (u * TAPS + t) % R
                    act.wait_ge(staged, s + 1)
                    act.wait_ge(gathered[u][t], 16 * (r + 1))
                    wait(act, turned, n - R + 1)
                    nc.scalar.activation(blend[:, slot, :], pix[:, u, t, 0:C], ACT.Copy,
                                         scale=part[:, u, t, 0:1]).then_inc(first_corner, 1)

                def step(s, r, u):
                    for t in range(TAPS):
                        n = s * TAPS + t
                        if t < TAPS - 1:
                            first(s, r, u, t + 1)
                        elif not (isinstance(s, int) and s == TILES - 1):
                            first(s + 1, r + u, 1 - u, 0)
                        act.wait_ge(turned, n + 1)
                        wait(act, multiplied, n - 1)
                        nc.scalar.activation(bT[:, (u * TAPS + t) % 2], psum[:, (u * TAPS + t) % 2, 0:C]
                                             .rearrange("p (k n) -> p k n", k=KC), ACT.Copy).then_inc(bT_copied, 1)
                        if t == 4 and not (isinstance(s, int) and s == 0):
                            finish(s - 1, r + u - 1, 1 - u)

                def finish(s, r, u):
                    act.wait_ge(scaled, 2 * s + 2)
                    wait(act, stored[u], 16 * r)
                    nc.scalar.activation(y[:, u, :], y2[:, u, :], ACT.Relu).then_inc(finished, 1)

                act.wait_ge(weights, constants.count)
                act.wait_ge(eps_set, 1)
                nc.scalar.activation(std_r[:], std_r[:], ACT.Sqrt, bias=eps[:]).then_inc(rooted, 1)
                first(0, 0, 0, 0)
                turns(act, TILES, step, head=2)
                finish(TILES - 1, TILES // 2 - 1, 1)

            @block.tensor
            def _(pe):
                def turn(s, u, t):
                    n = s * TAPS + t
                    pe.wait_ge(blended, n + 1)
                    wait(pe, bT_copied, n - 1)
                    for k in range(KC):
                        m = nc.tensor.transpose(psum[:, (u * TAPS + t) % 2, k * P:(k + 1) * P],
                                                blend[:, (u * TAPS + t) % R, k * P:(k + 1) * P], chip.ident[:])
                    m.then_inc(turned, 1)

                def step(s, r, u):
                    for t in range(TAPS):
                        if t < TAPS - 1:
                            turn(s, u, t + 1)
                        elif not (isinstance(s, int) and s == TILES - 1):
                            turn(s + 1, 1 - u, 0)
                        pe.wait_ge(bT_copied, s * TAPS + t + 1)
                        if t == 0:
                            wait(pe, centred, s - 1)
                        for k in range(KC):
                            m = nc.tensor.matmul(psum[:, 4 + u, 0:C], bT[:, (u * TAPS + t) % 2, k, :], w[:, t, k, :],
                                                 start=(t == 0 and k == 0), stop=(t == TAPS - 1 and k == KC - 1))
                        m.then_inc(multiplied, 1)

                pe.wait_ge(weights, constants.count)
                turn(0, 0, 0)
                turns(pe, TILES, step)


def conv_sequence(nc, x, wq, wk, wv1, wv2, wo, w1, b1, w2, b2, g_agg, be_agg, g_out, be_out,
                  kernel_f, kernel_g, kernel_h, gamma,
                  wq2, bq, wk2, bk, wv, bv, wcq, bcq, wck, bck, wcv, bcv, wp, bp,
                  offset_w, dcn_w, bn_gamma, bn_beta, mean, var, out):
    def scratch(name, shape):
        return nc.dram_tensor(name + "_dram", shape, F32, kind="Internal").ap()

    v2_dram, e_dram, r_dram = scratch("v2", [N, P, C]), scratch("e", [B, N, N, BANK]), scratch("r", [B, N, BANK])
    x1, fg, h = scratch("x1", [B, N, N, C]), scratch("fg", [2 * D, B, N, N]), scratch("h", [B, N, N, C])
    x2, qkc, v, mix_dram = scratch("x2", [B, HW, C]), scratch("qkc", [3 * D, T]), scratch("v", [T, C]), scratch("mix", [D, B, C])
    corners, padded = scratch("corners", [B, S1, S1, 4, C]), scratch("padded", [B, S2, S2, C])
    fg_parts = fg.rearrange("(a r) b y x -> a r b (y x)", a=2)
    qkc_parts = qkc.rearrange("(a r) (b n) -> a r b n", a=3, b=B)

    def load_gamma(sp, gam, mix, sem):
        sp.dma_start(gam[:], across(gamma)).then_inc(sem, 16)

    def load_mix(sp, gam, mix, sem):
        sp.dma_start(mix[:], mix_dram).then_inc(sem, 16)

    def store_x2(sp, b, t, y_slot, sem):
        sp.dma_start(x2[b, bass.ds(t * QT, QT), :].rearrange("(j p) c -> p j c", p=P), y_slot).then_inc(sem, 16)

    load_gamma.count = load_mix.count = store_x2.count = 1

    with ExitStack() as ctx:
        chip = Chip(nc, ctx)
        with nc.cleanup_on_exit():
            make_identity(nc, chip)
            clear_borders(nc, chip, corners, padded)
            triangle_scores(nc, chip, x, wq, wk, wv2, v2_dram, e_dram, r_dram)
        with nc.cleanup_on_exit():
            triangle_output(nc, chip, x, wv1, wo, w1, b1, w2, b2, g_agg, be_agg, g_out, be_out, (kernel_f, kernel_g),
                            kernel_h, v2_dram, e_dram, r_dram, x1, fg, h)
        with nc.cleanup_on_exit():
            attention(nc, chip, "attention1", fg_parts[0], fg_parts[1], h.rearrange("b y x c -> b (y x) c"),
                      x1.rearrange("b y x c -> b (y x) c"), 1.0, True, None, load_gamma, store_x2)
        with nc.cleanup_on_exit():
            project2(nc, chip, x2.rearrange("b n c -> (b n) c"), wq2, bq, wk2, bk, wv, bv, wcq, bcq, wck, bck, wcv, bcv,
                     wp, bp, qkc, v, mix_dram)
        with nc.cleanup_on_exit():
            attention(nc, chip, "attention2", qkc_parts[1], qkc_parts[0], v.rearrange("(b n) c -> b n c", b=B), x2,
                      float(CR) ** -0.5, False, qkc_parts[2], load_mix, corner_store(corners, padded))
        with nc.sbuf_tensor("off_all", [P, TILES, OQ], F32) as off_all, \
                nc.sbuf_tensor("place", [P, TILES, TAPS], F32) as place, \
                nc.sbuf_tensor("weight", [P, TILES, TAPS, 4], F32) as weight:
            with nc.cleanup_on_exit(), ExitStack() as kept:
                constants = SamplingConstants(nc, chip, kept, dcn_w, bn_gamma, bn_beta, mean, var)
                offsets(nc, chip, padded, offset_w, off_all, constants.load)
                sample_plan(nc, chip, off_all, place, weight)
                deformable(nc, chip, corners, constants, place, weight, out)


_INS = ['x', 'L0_conv_Wq', 'L0_conv_Wk', 'L0_conv_Wv1', 'L0_conv_Wv2', 'L0_conv_Wo', 'L0_conv_W1', 'L0_conv_b1',
        'L0_conv_W2', 'L0_conv_b2', 'L0_conv_g_agg', 'L0_conv_be_agg', 'L0_conv_g_out', 'L0_conv_be_out',
        'L1_conv_kernel_f', 'L1_conv_kernel_g', 'L1_conv_kernel_h', 'L1_conv_gamma',
        'L2_conv_Wq', 'L2_conv_bq', 'L2_conv_Wk', 'L2_conv_bk', 'L2_conv_Wv', 'L2_conv_bv', 'L2_conv_Wcq', 'L2_conv_bcq',
        'L2_conv_Wck', 'L2_conv_bck', 'L2_conv_Wcv', 'L2_conv_bcv', 'L2_conv_Wp', 'L2_conv_bp',
        'L3_conv_offset_w', 'L3_conv_dcn_w', 'L3_conv_gamma', 'L3_conv_beta', 'L3_conv_moving_mean', 'L3_conv_moving_var']
_OUTS = [((B, N, N, C), 'float32')]


def kernel(**inputs):
    import numpy as _np
    import concourse.bacc as _bacc
    from concourse import mybir as _mybir
    from concourse.bass_utils import run_bass_kernel_spmd as _run

    nc = _bacc.Bacc("TRN2", target_bir_lowering=False, num_devices=1)
    arrays, args = {}, []
    for name in _INS:
        a = _np.ascontiguousarray(inputs[name])
        arrays[f"in_{name}_dram"] = a
        args.append(nc.dram_tensor(f"in_{name}_dram", a.shape, _mybir.dt.from_np(a.dtype), kind="ExternalInput").ap())
    for i, (shape, dtype) in enumerate(_OUTS):
        dt = _mybir.dt.from_np(_np.dtype(dtype))
        args.append(nc.dram_tensor(f"out_{i}_dram", shape, dt, kind="ExternalOutput").ap())
    conv_sequence(nc, *args)
    r = _run(nc, [arrays], core_ids=[0])
    got = tuple(r.results[0][f"out_{i}_dram"] for i in range(len(_OUTS)))
    return got[0]
```
